# Optimizing a Trainium2 kernel written in Bass

```python
import numpy as np
import jax
import jax.numpy as jnp

def _softmax(x, axis=-1):
    return jax.nn.softmax(x, axis=axis)

def _gelu(x):
    return jax.nn.gelu(x, approximate=True)

def _silu(x):
    return jax.nn.silu(x)

def _sigmoid(x):
    return jax.nn.sigmoid(x)

def _layernorm(x, axis=-1, eps=1e-05):
    m = jnp.mean(x, axis=axis, keepdims=True)
    v = jnp.var(x, axis=axis, keepdims=True)
    return (x - m) / jnp.sqrt(v + eps)

def _scatter_add(tgt, idx, src, axis=0):
    return tgt.at[idx].add(src)

def _segment_sum(src, seg, n):
    return jax.ops.segment_sum(src, seg, n)
kernel_name = 'mk_adj_preln_d2_adj_r2_bc7299'

def setup_inputs(seed: int=0):
    np.random.seed(seed)
    _w = jnp.asarray

    def _rec_inputs():
        import jax
        import jax.numpy as jnp
        _gk = jax.random.key(seed)
        x = -0.001547 + 1.001 * jax.random.normal(jax.random.fold_in(_gk, 1), (128, 128, 256), jnp.float32)
        _w = (1.0 + jnp.arange(128, dtype=jnp.float32)) ** (-0.5)
        _w = _w / _w.mean()
        _pij = jnp.clip(0.0625 * _w[:, None] * _w[None, :], 0.0, 1.0)
        _a = jax.random.uniform(jax.random.fold_in(_gk, 2), (128, 128)) < _pij
        _a = jnp.logical_or(_a, jnp.swapaxes(_a, -1, -2))
        _a = jnp.logical_or(_a, jnp.eye(128, dtype=bool))
        _af = _a.astype(jnp.float32)
        _af = _af * jax.random.uniform(jax.random.fold_in(_gk, 3), (128, 128), jnp.float32, 0.05, 0.237401)
        adj = _af
        return (x, adj)
    x, adj = _rec_inputs()

    def _L0_gnn_setup():
        import jax, jax.numpy as jnp
        import numpy as np
        key = jax.random.key(seed)
        k1, k2, k3, k4 = jax.random.split(key, 4)
        B, D, N = (4, 128, 256)
        scale = 1.0 / np.sqrt(2 * D)
        x = jax.random.normal(k1, (B, D, N), dtype=jnp.float32)
        W1 = jax.random.normal(k2, (D, D), dtype=jnp.float32) * scale
        W2 = jax.random.normal(k3, (D, D), dtype=jnp.float32) * scale
        b = jax.random.normal(k4, (D,), dtype=jnp.float32) * scale
        return {'x': x, 'W1': W1, 'W2': W2, 'b': b}
    _L0_gnn_all = _L0_gnn_setup()
    _L0_gnn_in = {k: v for k, v in _L0_gnn_all.items() if k in ('b',)}
    del _L0_gnn_all

    def _L1_gnn_setup():
        import jax, jax.numpy as jnp
        import numpy as np
        B, N, D, H = (16, 1025, 256, 8)
        LN_EPS = 1e-05

        def _make_mask(key, n):
            n_proto = n - 1
            adj = jax.random.bernoulli(key, 0.03, (n_proto, n_proto)).astype(jnp.float32)
            adj = jnp.clip(adj + adj.T + jnp.eye(n_proto, dtype=jnp.float32), 0.0, 1.0)
            mask = jnp.zeros((n, n), dtype=jnp.float32)
            mask = mask.at[0, :].set(1.0).at[:, 0].set(1.0)
            mask = mask.at[1:, 1:].set(adj)
            return mask
        key = jax.random.key(seed)
        ks = jax.random.split(key, 7)
        s = 1.0 / np.sqrt(D)
        return {'x': jax.random.normal(ks[0], (B, N, D), dtype=jnp.float32), 'w_qkv': jax.random.uniform(ks[1], (D, 3 * D), dtype=jnp.float32, minval=-s, maxval=s), 'w_proj': jax.random.uniform(ks[2], (D, D), dtype=jnp.float32, minval=-s, maxval=s), 'b_proj': jnp.zeros((D,), dtype=jnp.float32), 'ln_gamma': jnp.ones((D,), dtype=jnp.float32), 'ln_beta': jnp.zeros((D,), dtype=jnp.float32), 'attn_mask': _make_mask(ks[3], N)}
    _L1_gnn_all = _L1_gnn_setup()
    _L1_gnn_in = {k: v for k, v in _L1_gnn_all.items() if k in ('w_qkv', 'w_proj', 'b_proj', 'ln_gamma', 'ln_beta')}
    del _L1_gnn_all
    return {'x': x, 'adj': adj, 'L0_gnn_b': _L0_gnn_in['b'], 'L1_gnn_w_qkv': _L1_gnn_in['w_qkv'], 'L1_gnn_w_proj': _L1_gnn_in['w_proj'], 'L1_gnn_b_proj': _L1_gnn_in['b_proj'], 'L1_gnn_ln_gamma': _L1_gnn_in['ln_gamma'], 'L1_gnn_ln_beta': _L1_gnn_in['ln_beta']}

def reference(x, adj, L0_gnn_b, L1_gnn_w_qkv, L1_gnn_w_proj, L1_gnn_b_proj, L1_gnn_ln_gamma, L1_gnn_ln_beta):
    import jax
    import jax.numpy as jnp

    def _L0_gnn_ref(x, W1, W2, b):
        import jax, jax.numpy as jnp
        import numpy as np
        A = jnp.einsum('od,bdn->bon', W1, x)
        C = jnp.einsum('od,bdn->bon', W2, x) + b[None, :, None]
        pre = A[:, :, None, :] + (C - A)[:, :, :, None]
        out = jnp.max(jax.nn.relu(pre), axis=-1)
        return out

    def _L1_gnn_ref(x, w_qkv, w_proj, b_proj, ln_gamma, ln_beta, attn_mask):
        import jax, jax.numpy as jnp
        import numpy as np
        B, N, D, H = (16, 1025, 256, 8)
        LN_EPS = 1e-05

        def _make_mask(key, n):
            n_proto = n - 1
            adj = jax.random.bernoulli(key, 0.03, (n_proto, n_proto)).astype(jnp.float32)
            adj = jnp.clip(adj + adj.T + jnp.eye(n_proto, dtype=jnp.float32), 0.0, 1.0)
            mask = jnp.zeros((n, n), dtype=jnp.float32)
            mask = mask.at[0, :].set(1.0).at[:, 0].set(1.0)
            mask = mask.at[1:, 1:].set(adj)
            return mask
        b, n, d = x.shape
        hd = d // H
        scale = hd ** (-0.5)
        qkv = (x @ w_qkv).reshape(b, n, 3, H, hd).transpose(2, 0, 3, 1, 4)
        q, k, v = (qkv[0], qkv[1], qkv[2])
        attn = jnp.einsum('bhnd,bhmd->bhnm', q, k) * scale
        attn = jnp.where(attn_mask[None, None] == 0, -jnp.inf, attn)
        attn = jax.nn.softmax(attn, axis=-1)
        o = jnp.einsum('bhnm,bhmd->bhnd', attn, v).transpose(0, 2, 1, 3).reshape(b, n, d)
        o = o @ w_proj + b_proj
        mu = jnp.mean(o, axis=-1, keepdims=True)
        var = jnp.mean(jnp.square(o - mu), axis=-1, keepdims=True)
        ln = (o - mu) * jax.lax.rsqrt(var + LN_EPS) * ln_gamma + ln_beta
        return o + ln
    h = jnp.maximum(_layernorm(x, axis=-1), 0.0)
    x = x + _L0_gnn_ref(h, adj, adj, L0_gnn_b)
    h = jnp.maximum(_layernorm(x, axis=-1), 0.0)
    x = x + _L1_gnn_ref(h, L1_gnn_w_qkv, L1_gnn_w_proj, L1_gnn_b_proj, L1_gnn_ln_gamma, L1_gnn_ln_beta, adj)
    return x

_drawn_inputs = setup_inputs


def setup_inputs(seed=0):
    import zlib

    import numpy as np

    out = dict(_drawn_inputs(seed))
    spreads = {'L1_gnn_b_proj': (0.0, 0.1), 'L1_gnn_ln_gamma': (1.0, 0.2), 'L1_gnn_ln_beta': (0.0, 0.1)}
    factors = {}
    for name, (base, spread) in spreads.items():
        noise = np.random.default_rng([zlib.crc32(name.encode()), seed]).standard_normal(out[name].shape)
        drawn = base * np.exp(spread * noise) if base else spread * noise
        out[name] = jnp.asarray(drawn.astype(out[name].dtype))
    for name, factor in factors.items():
        out[name] = (out[name] * factor).astype(out[name].dtype)
    return out
```

```python
from contextlib import ExitStack

import numpy as np
import concourse.bass as bass
from concourse import mybir

B, N, D = 128, 128, 256
H, HD = 8, 32
G = 4
STEPS = B // G
P = 128
DC = D // P
HC = P // HD
UNITS = G * DC
STACK = 3 * HD
ROWS = STACK + 2
WS = 16.0
MS = 32.0
MASKED = -1e30
SCALE = float(HD) ** -0.5 / (WS * WS)
EPS = 1e-5
SC_SLOTS = 3
P_SLOTS = 4
PAIRS = 4 * DC * G * N
DMAS = 3 * H


def build(nc, x, adj, bias0, w_qkv, w_proj, b_proj, gamma, beta, out):
    F32, F16, BF16 = mybir.dt.float32, mybir.dt.float16, mybir.dt.bfloat16
    ALU, ACT, AX = mybir.AluOpType, mybir.ActivationFunctionType, mybir.AxisListType

    with ExitStack() as ctx:
        def sb(name, shape, dt=F32):
            return ctx.enter_context(nc.sbuf_tensor(name, shape, dt))

        def ps(name, shape, dt=F32):
            return ctx.enter_context(nc.psum_tensor(name, shape, dt))

        def sem(name):
            return ctx.enter_context(nc.semaphore(name))

        adj_sb = sb("adj_sb", [P, N])
        w_sb = sb("w_sb", [P, DC, 3 * D])
        wp_sb = sb("wp_sb", [P, DC, D])
        gamma_sb = sb("gamma_sb", [P, D])
        beta_sb = sb("beta_sb", [P, D])
        bproj_sb = sb("bproj_sb", [P, D])
        bproj_r1 = sb("bproj_r1", [P, D])
        bproj_r2 = sb("bproj_r2", [P, D])
        bias0_sb = sb("bias0_sb", [P, 1])
        w_hi = sb("w_hi", [P, DC, 3 * D], F16)
        w_lo = sb("w_lo", [P, DC, 3 * D], F16)
        adjT_hi = sb("adjT_hi", [P, N], F16)
        adjT_lo = sb("adjT_lo", [P, N], F16)
        mask_q = sb("mask_q", [P, HC, N], BF16)
        mask_k = sb("mask_k", [P, HC, N], BF16)
        bp_parts = sb("bp_parts", [P, 3, D], F16)
        bp_rows = sb("bp_rows", [P, D], F16)
        ones16 = sb("ones16", [P, P], F16)
        identf = sb("identf", [P, P])
        ident16 = sb("ident16", [P, P], F16)
        identb = sb("identb", [P, P], BF16)
        sel_sum = sb("sel_sum", [P, UNITS, HD])
        sel_row = sb("sel_row", [P, UNITS, HC, HD])
        mhalf = sb("mhalf", [P, G])
        dve_cell = sb("dve_cell", [P, 2])
        pool_cell = sb("pool_cell", [P, 4])
        x_sb = sb("x_sb", [P, 2, G, D])
        y_sb = sb("y_sb", [P, 2, G, D])
        st1 = sb("st1", [P, G, 6])
        mv1 = sb("mv1", [P, G, 2])
        negm1 = sb("negm1", [P, G])
        ve1 = sb("ve1", [P, G])
        rstd1 = sb("rstd1", [P, G])
        z_sb = sb("z_sb", [P, G, D])
        h_hi = sb("h_hi", [P, G, D], F16)
        h_lo = sb("h_lo", [P, G, D], F16)
        hT = sb("hT", [P, 2, DC, G, N], F16)
        amax = sb("amax", [P, G])
        l0 = sb("l0", [P, 2, G])
        v_sb = sb("v_sb", [P, 2, G, D])
        pairs = sb("pairs", [P, 2, DC, 2, G * N], F16)
        stack = sb("stack", [P, 2, 2, H, G, N], F16)
        smax = sb("smax", [P, H, G])
        crow = sb("crow", [H * G, 2, N], F16)
        p_sb = sb("p_sb", [P, P_SLOTS, HC, N])
        pv_sb = sb("pv_sb", [P, G, DC, N])
        rsum = sb("rsum", [P, N])
        oT = sb("oT", [P, G, DC, N])
        o_sb = sb("o_sb", [P, G, D])
        st2 = sb("st2", [P, G, 6])
        mv2 = sb("mv2", [P, G, 2])
        ve2 = sb("ve2", [P, G])
        rstd2 = sb("rstd2", [P, G])
        negm2 = sb("negm2", [P, G])
        nb2 = sb("nb2", [P, G])
        t_sb = sb("t_sb", [P, G, D])

        sc_ps = [ps(f"sc_ps{i}", [P, HC, N]) for i in range(SC_SLOTS)]
        a_ps = [ps(f"a_ps{i}", [P, G * N]) for i in range(2)]
        sum_ps = ps("sum_ps", [P, 4, N])
        pv_ps = ps("pv_ps", [P, 2 * DC, N])
        ro_ps = ps("ro_ps", [P, 2, D])

        c_load = sem("c_load")
        pool_const = sem("pool_const")
        act_const = sem("act_const")
        dve_const = sem("dve_const")
        adjT_ps = sem("adjT_ps")
        x_loaded = sem("x_loaded")
        stats1 = sem("stats1")
        mv1_ready = sem("mv1_ready")
        norm1 = sem("norm1")
        z_ready = sem("z_ready")
        hhi_ready = sem("hhi_ready")
        hlo_ready = sem("hlo_ready")
        hT_psum = sem("hT_psum")
        hT_ready = sem("hT_ready")
        a_psum = sem("a_psum")
        amax_ready = sem("amax_ready")
        l0_ready = sem("l0_ready")
        v_psum = sem("v_psum")
        v_ready = sem("v_ready")
        qk_psum = sem("qk_psum")
        qkhi_ready = sem("qkhi_ready")
        qklo_ready = sem("qklo_ready")
        stacked = sem("stacked")
        s_psum = sem("s_psum")
        smax_ready = sem("smax_ready")
        maxT_psum = sem("maxT_psum")
        chi_ready = sem("chi_ready")
        clo_ready = sem("clo_ready")
        crow_in = sem("crow_in")
        st_psum = sem("st_psum")
        p_ready = sem("p_ready")
        pv_psum = sem("pv_psum")
        pv_ready = sem("pv_ready")
        rsum_ready = sem("rsum_ready")
        r_psum = sem("r_psum")
        oT_ready = sem("oT_ready")
        o_psum = sem("o_psum")
        o_ready = sem("o_ready")
        stats2 = sem("stats2")
        mv2_ready = sem("mv2_ready")
        norm2 = sem("norm2")
        t_ready = sem("t_ready")
        y_init = sem("y_init")
        y_beta = sem("y_beta")
        y_o = sem("y_o")
        tg_ready = sem("tg_ready")
        y_ready = sem("y_ready")
        stored = sem("stored")
        pool_zero = sem("pool_zero")

        xg = x.rearrange("(g b) n d -> g n b d", b=G)
        og = out.rearrange("(g b) n d -> g n b d", b=G)

        def wait(eng, s, value):
            if not isinstance(value, int) or value > 0:
                eng.wait_ge(s, value)

        def pipeline(eng, step):
            step(0, 0, True, False, False, True)
            step(1, 1, True, True, False, True)
            with eng.Fori(2, STEPS - 2, 2) as t:
                step(t, 0, True, True, True, True)
                step(t + 1, 1, True, True, True, True)
            step(STEPS - 2, 0, True, True, True, True)
            step(STEPS - 1, 1, True, True, True, False)
            step(STEPS, 0, False, True, True, False)
            step(STEPS + 1, 1, False, False, True, False)

        block = ctx.enter_context(nc.Block())

        @block.sync
        def _(sp):
            nc.sync.dma_start(x_sb[:, 0], xg[0]).then_inc(x_loaded, 16)
            nc.sync.dma_start(adj_sb[:], adj).then_inc(c_load, 16)
            nc.sync.dma_start(w_sb[:], w_qkv.rearrange("(c p) n -> p c n", p=P)).then_inc(c_load, 16)
            nc.sync.dma_start(wp_sb[:], w_proj.rearrange("(c p) n -> p c n", p=P)).then_inc(c_load, 16)
            nc.sync.dma_start(bias0_sb[:], bias0.rearrange("(p o) -> p o", o=1)).then_inc(c_load, 16)
            for vec, dst in ((gamma, gamma_sb), (beta, beta_sb), (b_proj, bproj_sb)):
                nc.sync.dma_start(dst[:], vec.rearrange("(o d) -> o d", o=1).to_broadcast([P, D])).then_inc(c_load, 16)

            def step(t, par, a, bc, d, prep):
                if bc:
                    for part, done in enumerate((chi_ready, clo_ready)):
                        sp.wait_ge(done, t)
                        row = stack[STACK + part:STACK + part + 1, 1 - par, 0].rearrange("p h b n -> p (h b) n")
                        nc.sync.dma_start(row, crow[:, part]).then_inc(crow_in, 16)
                if a:
                    for j in range(DC):
                        if j == 0:
                            wait(sp, st_psum, UNITS * (t - 1))
                        both = sp.snap(4 * t + 2 * j + 2) if not isinstance(t, int) else 4 * t + 2 * j + 2
                        wait(sp, qkhi_ready, both)
                        wait(sp, qklo_ready, both)
                        for i in range(HC):
                            head = slice(HD * i, HD * (i + 1))
                            high = bass.AP(pairs[:].tensor, HD * i * PAIRS + 2 * j * G * N,
                                           [[PAIRS, HD], [(2 * DC + 1) * G * N, 2], [1, G * N]])
                            for blk, src in enumerate((high, pairs[head, 0, j], pairs[head, 1, j])):
                                dst = stack[blk * HD:(blk + 1) * HD, par, :, HC * j + i]
                                nc.sync.dma_start(dst.rearrange("p s b n -> p s (b n)"), src).then_inc(stacked, 16)

            pipeline(sp, step)

        @block.tensor
        def _(pe):
            pe.wait_ge(c_load, 16 * 7)
            pe.wait_ge(pool_const, 1)
            nc.tensor.transpose(sc_ps[0][:, 0, :], adj_sb[:], identf[:]).then_inc(adjT_ps, 1)
            pe.wait_ge(pool_const, 5)
            pe.wait_ge(dve_const, DVE_CONST)
            pe.wait_ge(act_const, ACT_CONST)

            def transpose_h(t, b):
                pe.wait_ge(hhi_ready, 4 * t + b + 1)
                pe.wait_ge(hlo_ready, 4 * t + b + 1)
                if b < 2:
                    wait(pe, v_ready, 2 * t - 1 + b)
                else:
                    pe.wait_ge(hT_ready, 4 * t + b - 1)
                to = a_ps[b % 2][:].bitcast(F16)
                for i, (h, c) in enumerate(((h_hi, 0), (h_hi, 1), (h_lo, 0), (h_lo, 1))):
                    mm = nc.tensor.transpose(to[:, i * N:(i + 1) * N], h[:, b, c * P:(c + 1) * P], ident16[:])
                mm.then_inc(hT_psum, 1)

            def layer0(t, i):
                pe.wait_ge(hT_ready, 4 * t + 3 + i)
                for k, (w, h) in enumerate(((adjT_hi, h_hi), (adjT_hi, h_lo), (adjT_lo, h_hi))):
                    mm = nc.tensor.matmul(a_ps[i][:], w[:], h[:, 2 * i:2 * i + 2].rearrange("p b d -> p (b d)"),
                                          start=(k == 0), stop=(k == 2))
                mm.then_inc(a_psum, 1)

            def project_qk(t, c):
                if c == 0:
                    pe.wait_ge(hT_ready, 4 * t + 4)
                if c < 2:
                    pe.wait_ge(amax_ready, 2 * t + c + 1)
                else:
                    pe.wait_ge(qkhi_ready, 4 * t + c - 1)
                    pe.wait_ge(qklo_ready, 4 * t + c - 1)
                col = (c % 2) * D + (c // 2) * P
                k = 0
                for w, part in ((w_hi, 0), (w_hi, 1), (w_lo, 0)):
                    for dc in range(DC):
                        mm = nc.tensor.matmul(a_ps[c % 2][:], w[:, dc, col:col + P],
                                              hT[:, part, dc].rearrange("p b n -> p (b n)"),
                                              start=(k == 0), stop=(k == 5))
                        k += 1
                mm.then_inc(qk_psum, 1)

            def project_v(t, i):
                pe.wait_ge(qkhi_ready, 4 * t + 3 + i)
                pe.wait_ge(qklo_ready, 4 * t + 3 + i)
                for bb in range(2):
                    k = 0
                    for part, w in ((0, w_hi), (1, w_hi), (0, w_lo)):
                        for dc in range(DC):
                            mm = nc.tensor.matmul(a_ps[i][:, bb * D:(bb + 1) * D], hT[:, part, dc, 2 * i + bb],
                                                  w[:, dc, 2 * D:3 * D], start=(k == 0), stop=(k == 5))
                            k += 1
                mm.then_inc(v_psum, 1)

            def scores(g, par, u):
                b, j = u // DC, u % DC
                if u == 0:
                    pe.wait_ge(stacked, 16 * DMAS * (g + 1))
                if u < SC_SLOTS:
                    wait(pe, p_ready, UNITS * (g - 1) + (8, 6, 7)[u])
                else:
                    pe.wait_ge(smax_ready, UNITS * g + u - SC_SLOTS + 1)
                to = sc_ps[u % SC_SLOTS]
                nc.tensor.matmul(to[:].rearrange("p h n -> p (h n)"), identb[:],
                                 mask_q[:].rearrange("p h n -> p (h n)"), start=True, stop=False, skip_group_check=True)
                for i in range(HC):
                    h = HC * j + i
                    mm = nc.tensor.matmul(to[:, i], stack[0:STACK, par, 0, h, b], stack[0:STACK, par, 1, h, b],
                                          start=False, stop=True, skip_group_check=True)
                mm.then_inc(s_psum, 1)

            def transpose_max(g):
                pe.wait_ge(smax_ready, UNITS * (g + 1))
                wait(pe, rsum_ready, g)
                nc.tensor.transpose(sum_ps[0:H * G, 1, :], smax[:].rearrange("p h b -> p (h b)"),
                                    identf[:]).then_inc(maxT_psum, 1)

            def scores_T(g, par, u):
                b, j = u // DC, u % DC
                if u == 0:
                    pe.wait_ge(crow_in, 32 * (g + 1))
                if u < SC_SLOTS:
                    pe.wait_ge(smax_ready, UNITS * g + 6 + u)
                else:
                    pe.wait_ge(p_ready, UNITS * g + u - SC_SLOTS + 1)
                to = sc_ps[(UNITS + u) % SC_SLOTS]
                nc.tensor.matmul(to[:].rearrange("p h n -> p (h n)"), identb[:],
                                 mask_k[:].rearrange("p h n -> p (h n)"), start=True, stop=False, skip_group_check=True)
                for i in range(HC):
                    h = HC * j + i
                    mm = nc.tensor.matmul(to[:, i], stack[0:ROWS, par, 1, h, b], stack[0:ROWS, par, 0, h, b],
                                          start=False, stop=True, skip_group_check=True)
                mm.then_inc(st_psum, 1)

            def values(g, par, u):
                b, j = u // DC, u % DC
                pe.wait_ge(p_ready, UNITS * g + u + 1)
                if j == 0:
                    if b % 2 == 0:
                        pe.wait_ge(v_ready, 2 * g + b // 2 + 1)
                    wait(pe, pv_ready, G * g + b)
                if u == 0:
                    wait(pe, rsum_ready, g)
                    pe.wait_ge(clo_ready, g + 1)
                for i in range(HC):
                    h = HC * j + i
                    nc.tensor.matmul(pv_ps[HD * i:HD * (i + 1), j], v_sb[:, par, b, HD * h:HD * (h + 1)],
                                     p_sb[:, u % P_SLOTS, i], start=True, stop=True)
                for i in range(HC):
                    mm = nc.tensor.matmul(sum_ps[HD * i:HD * (i + 1), 0], sel_sum[:, u], p_sb[:, u % P_SLOTS, i],
                                          start=(u == 0), stop=(u == UNITS - 1), skip_group_check=True)
                mm.then_inc(pv_psum, 1)

            def spread(g, b):
                if b == 0:
                    pe.wait_ge(rsum_ready, g + 1)
                wait(pe, o_ready, G * g + b)
                for j in range(DC):
                    mm = nc.tensor.matmul(ro_ps[:, 0, j * N:(j + 1) * N],
                                          sel_row[:, b * DC + j].rearrange("p h d -> p (h d)"), rsum[:],
                                          start=True, stop=True)
                mm.then_inc(r_psum, 1)

            def project_o(g, b):
                pe.wait_ge(oT_ready, G * g + b + 1)
                nc.tensor.matmul(ro_ps[:, 1], ones16[:], bp_rows[:], start=True, stop=False)
                for j in range(DC):
                    mm = nc.tensor.matmul(ro_ps[:, 1], oT[:, b, j], wp_sb[:, j], start=False, stop=(j == DC - 1))
                mm.then_inc(o_psum, 1)

            ORDER = ("S0 T0 S1 R0 S2 T1 S3 O0 S4 T2 R1 S5 T3 O1 S6 R2 S7 L0 O2 M0 Q0 R3 L1 O3 "
                     "E0 E1 Q1 P0 P1 E2 Q2 E3 P2 P3 E4 Q3 E5 P4 P5 V0 E6 E7 P6 P7 V1").split()

            def step(t, par, a, bc, d, prep):
                for what in ORDER:
                    kind, i = what[0], int(what[1])
                    if kind == "T" and a:
                        transpose_h(t, i)
                    elif kind == "L" and a:
                        layer0(t, i)
                    elif kind == "Q" and a:
                        project_qk(t, i)
                    elif kind == "V" and a:
                        project_v(t, i)
                    elif kind == "S" and bc:
                        scores(t - 1, 1 - par, i)
                    elif kind == "M" and bc:
                        transpose_max(t - 1)
                    elif kind == "E" and bc:
                        scores_T(t - 1, 1 - par, i)
                    elif kind == "P" and bc:
                        values(t - 1, 1 - par, i)
                    elif kind == "R" and d:
                        spread(t - 2, i)
                    elif kind == "O" and d:
                        project_o(t - 2, i)

            pipeline(pe, step)

        @block.scalar
        def _(act):
            act.wait_ge(c_load, 16 * 7)
            nc.scalar.activation(w_hi[:], w_sb[:], ACT.Copy, scale=WS).then_inc(act_const, 1)
            nc.scalar.activation(bp_parts[:, 0], bproj_sb[:], ACT.Copy).then_inc(act_const, 1)
            act.wait_ge(adjT_ps, 1)
            nc.scalar.activation(adjT_hi[:], sc_ps[0][:, 0, :], ACT.Copy, scale=WS).then_inc(act_const, 1)

            def h_high(t, b):
                act.wait_ge(z_ready, G * t + b + 1)
                if b == 0:
                    wait(act, a_psum, 2 * t)
                    wait(act, hT_psum, G * t)
                nc.scalar.activation(h_hi[:, b], z_sb[:, b], ACT.Relu).then_inc(hhi_ready, 1)

            def take_hT(t, b):
                act.wait_ge(hT_psum, G * t + b + 1)
                if b == 0:
                    wait(act, v_psum, 2 * t)
                nc.scalar.activation(hT[:, :, :, b, :],
                                     a_ps[b % 2][:].bitcast(F16)[:, 0:4 * N].rearrange("p (s c n) -> p s c n", s=2, c=DC),
                                     ACT.Copy).then_inc(hT_ready, 1)

            def layer0_numbers(t, par):
                act.wait_ge(amax_ready, 2 * (t + 1))
                nc.scalar.activation(l0[:, par], amax[:], ACT.Relu, bias=bias0_sb[:, 0:1],
                                     scale=1.0 / WS).then_inc(l0_ready, 1)

            def start_y(g, par, b):
                if b == 0:
                    act.wait_ge(l0_ready, g + 1)
                    wait(act, stored, 16 * (g - 1))
                nc.scalar.activation(y_sb[:, par, b], x_sb[:, par, b], ACT.Identity,
                                     bias=l0[:, par, b:b + 1]).then_inc(y_init, 1)

            def load_x(t, par):
                wait(act, y_init, G * (t - 1))
                nc.scalar.dma_start(x_sb[:, par], xg[t]).then_inc(x_loaded, 16)

            def take_v(t, par, i):
                act.wait_ge(v_psum, 2 * t + i + 1)
                nc.scalar.activation(v_sb[:, par, 2 * i:2 * i + 2].rearrange("p b d -> p (b d)"), a_ps[i][:],
                                     ACT.Copy).then_inc(v_ready, 1)

            def qk_high(t, c):
                act.wait_ge(qk_psum, 4 * t + c + 1)
                if c == 0:
                    wait(act, stacked, 16 * DMAS * t)
                nc.scalar.activation(pairs[:, c % 2, c // 2, c % 2], a_ps[c % 2][:], ACT.Copy).then_inc(qkhi_ready, 1)

            def max_high(g):
                act.wait_ge(maxT_psum, g + 1)
                wait(act, crow_in, 32 * g)
                nc.scalar.activation(crow[:, 0], sum_ps[0:H * G, 1, :], ACT.Copy, scale=-1.0 / MS).then_inc(chi_ready, 1)

            def exps(g, u):
                act.wait_ge(st_psum, UNITS * g + u + 1)
                wait(act, pv_psum, UNITS * g + u - P_SLOTS + 1)
                nc.scalar.activation(p_sb[:, u % P_SLOTS], sc_ps[(UNITS + u) % SC_SLOTS][:], ACT.Exp,
                                     scale=SCALE).then_inc(p_ready, 1)

            def take_pv(g, b):
                act.wait_ge(pv_psum, UNITS * g + DC * (b + 1))
                if b == 0:
                    wait(act, oT_ready, G * g)
                nc.scalar.activation(pv_sb[:, b], pv_ps[:, 0:DC], ACT.Copy).then_inc(pv_ready, 1)

            def take_o(g, b):
                act.wait_ge(o_psum, G * g + b + 1)
                if b == 0:
                    wait(act, y_o, g)
                nc.scalar.activation(o_sb[:, b], ro_ps[:, 1], ACT.Copy).then_inc(o_ready, 1)

            def normalise_o(g, b):
                if b == 0:
                    act.wait_ge(norm2, 4 * (g + 1))
                    wait(act, y_ready, G * g)
                nc.scalar.activation(t_sb[:, b], o_sb[:, b], ACT.Identity, bias=nb2[:, b:b + 1],
                                     scale=rstd2[:, b:b + 1]).then_inc(t_ready, 1)

            ORDER = ("Y0 Y1 T0 Y2 T1 Y3 X0 O0 T2 T3 O1 O2 M0 Q0 O3 L0 "
                     "E0 E1 Q1 A0 E2 Q2 E3 A1 E4 Q3 E5 A2 N0 H0 N1 H1 V0 E6 E7 H2 N2 A3 V1 H3 N3").split()

            def step(t, par, a, bc, d, prep):
                for what in ORDER:
                    kind, i = what[0], int(what[1])
                    if kind == "Y" and bc:
                        start_y(t - 1, 1 - par, i)
                    elif kind == "T" and a:
                        take_hT(t, i)
                    elif kind == "L" and a:
                        layer0_numbers(t, par)
                    elif kind == "Q" and a:
                        qk_high(t, i)
                    elif kind == "V" and a:
                        take_v(t, par, i)
                    elif kind == "M" and bc:
                        max_high(t - 1)
                    elif kind == "E" and bc:
                        exps(t - 1, i)
                    elif kind == "A" and bc:
                        take_pv(t - 1, i)
                    elif kind == "O" and d:
                        take_o(t - 2, i)
                    elif kind == "N" and d:
                        normalise_o(t - 2, i)
                    elif kind == "X" and prep:
                        load_x(t + 1, 1 - par)
                    elif kind == "H" and prep:
                        h_high(t + 1, i)

            for b in range(G):
                h_high(0, b)
            pipeline(act, step)

        @block.vector
        def _(dve):
            nc.vector.memset(mhalf[:], -0.5).then_inc(dve_const, 1)
            nc.vector.memset(ones16[:], 1.0).then_inc(dve_const, 1)
            nc.vector.memset(bp_rows[:], 0.0).then_inc(dve_const, 1)
            for par in range(2):
                nc.vector.memset(stack[STACK:ROWS, par, 1], MS).then_inc(dve_const, 1)
            dve.wait_ge(c_load, 16 * 7)
            for i in range(HC):
                nc.vector.tensor_scalar(mask_q[:, i], adj_sb[:], 0.0, MASKED, ALU.is_equal, ALU.mult).then_inc(dve_const, 1)
            dve.wait_ge(act_const, 3)
            dve.wait_ge(adjT_ps, 1)
            for i in range(HC):
                nc.vector.tensor_scalar(mask_k[:, i], sc_ps[0][:, 0, :], 0.0, MASKED, ALU.is_equal, ALU.mult).then_inc(dve_const, 1)
            nc.vector.scalar_tensor_tensor(adjT_lo[:], sc_ps[0][:, 0, :], WS, adjT_hi[:], ALU.mult, ALU.subtract).then_inc(dve_const, 1)
            nc.vector.scalar_tensor_tensor(w_lo[:], w_sb[:], WS, w_hi[:], ALU.mult, ALU.subtract).then_inc(dve_const, 1)
            nc.vector.tensor_tensor(bproj_r1[:], bproj_sb[:], bp_parts[:, 0], ALU.subtract).then_inc(dve_const, 1)
            dve.wait_ge(dve_const, 16)
            nc.vector.tensor_copy(bp_parts[:, 1], bproj_r1[:]).then_inc(dve_const, 1)
            dve.wait_ge(dve_const, 17)
            nc.vector.tensor_tensor(bproj_r2[:], bproj_r1[:], bp_parts[:, 1], ALU.subtract).then_inc(dve_const, 1)
            dve.wait_ge(dve_const, 18)
            nc.vector.tensor_copy(bp_parts[:, 2], bproj_r2[:]).then_inc(dve_const, 1)
            dve.wait_ge(dve_const, 19)
            for i in range(3):
                nc.vector.tensor_copy(bp_rows[HD * i:HD * i + 1], bp_parts[HD * i:HD * i + 1, i]).then_inc(dve_const, 1)

            def stats_x(t, par):
                dve.wait_ge(x_loaded, 16 * (t + 1))
                wait(dve, mv1_ready, G * t)
                for b in range(G):
                    nc.vector.bn_stats(st1[:, b], x_sb[:, par, b]).then_inc(stats1, 1)
                dve.wait_ge(stats1, G * (t + 1))
                wait(dve, norm1, 3 * t)
                nc.vector.memset(dve_cell[:, 0:1], 0.0)
                for b in range(G):
                    nc.vector.bn_aggr(mv1[:, b], st1[:, b]).then_inc(mv1_ready, 1)

            def h_low(t, b):
                dve.wait_ge(hhi_ready, G * t + b + 1)
                if b == 0:
                    wait(dve, a_psum, 2 * t)
                nc.vector.scalar_tensor_tensor(h_lo[:, b], z_sb[:, b], 0.0, h_hi[:, b], ALU.max,
                                               ALU.subtract).then_inc(hlo_ready, 1)

            def layer0_max(t, i):
                dve.wait_ge(a_psum, 2 * t + i + 1)
                if i == 0:
                    wait(dve, l0_ready, t)
                nc.vector.tensor_reduce(amax[:, 2 * i:2 * i + 2], a_ps[i][:].rearrange("p (b d) -> p b d", b=2), AX.X,
                                        ALU.max).then_inc(amax_ready, 1)

            def qk_low(t, c):
                dve.wait_ge(qkhi_ready, 4 * t + c + 1)
                if c == 0:
                    wait(dve, stacked, 16 * DMAS * t)
                nc.vector.tensor_tensor(pairs[:, 1 - c % 2, c // 2, c % 2], a_ps[c % 2][:], pairs[:, c % 2, c // 2, c % 2],
                                        ALU.subtract).then_inc(qklo_ready, 1)

            def row_max(g, u):
                b, j = u // DC, u % DC
                dve.wait_ge(s_psum, UNITS * g + u + 1)
                if u == 0:
                    wait(dve, maxT_psum, g)
                nc.vector.tensor_reduce(smax[:, HC * j:HC * (j + 1), b], sc_ps[u % SC_SLOTS][:], AX.X,
                                        ALU.max).then_inc(smax_ready, 1)

            def max_low(g):
                dve.wait_ge(chi_ready, g + 1)
                wait(dve, crow_in, 32 * g)
                nc.vector.scalar_tensor_tensor(crow[:, 1], sum_ps[0:H * G, 1, :], -1.0 / MS, crow[:, 0], ALU.mult,
                                               ALU.subtract).then_inc(clo_ready, 1)

            def invert_sums(g):
                dve.wait_ge(pv_psum, UNITS * (g + 1))
                wait(dve, r_psum, G * g)
                nc.vector.reciprocal(rsum[:], sum_ps[:, 0, :]).then_inc(rsum_ready, 1)

            def scale_o(g, b):
                dve.wait_ge(r_psum, G * g + b + 1)
                dve.wait_ge(pv_ready, G * g + b + 1)
                if b == 0:
                    wait(dve, o_psum, G * g)
                nc.vector.tensor_tensor(oT[:, b].rearrange("p j n -> p (j n)"), ro_ps[:, 0],
                                        pv_sb[:, b].rearrange("p j n -> p (j n)"), ALU.mult).then_inc(oT_ready, 1)

            def stats_o(g, b):
                dve.wait_ge(o_ready, G * g + b + 1)
                nc.vector.bn_stats(st2[:, b], o_sb[:, b]).then_inc(stats2, 1)

            def aggregate_o(g):
                dve.wait_ge(stats2, G * (g + 1))
                wait(dve, norm2, 4 * g)
                nc.vector.memset(dve_cell[:, 1:2], 0.0)
                for b in range(G):
                    nc.vector.bn_aggr(mv2[:, b], st2[:, b]).then_inc(mv2_ready, 1)

            ORDER = ("I0 S0 S1 S2 O0 S3 S4 S5 O1 B0 S6 S7 O2 B1 L0 M0 X0 Q0 O3 B2 L1 B3 G0 Q1 "
                     "Q2 Q3 H0 H1 H2 H3").split()

            def step(t, par, a, bc, d, prep):
                for what in ORDER:
                    kind, i = what[0], int(what[1])
                    if kind == "I" and d:
                        invert_sums(t - 2)
                    elif kind == "O" and d:
                        scale_o(t - 2, i)
                    elif kind == "B" and d:
                        stats_o(t - 2, i)
                    elif kind == "G" and d:
                        aggregate_o(t - 2)
                    elif kind == "S" and bc:
                        row_max(t - 1, i)
                    elif kind == "M" and bc:
                        max_low(t - 1)
                    elif kind == "L" and a:
                        layer0_max(t, i)
                    elif kind == "Q" and a:
                        qk_low(t, i)
                    elif kind == "X" and prep:
                        stats_x(t + 1, 1 - par)
                    elif kind == "H" and prep:
                        h_low(t + 1, i)

            stats_x(0, 0)
            for b in range(G):
                h_low(0, b)
            pipeline(dve, step)

        @block.gpsimd
        def _(pool):
            for i, m in enumerate((identf, ident16, identb)):
                nc.gpsimd.memset(m[:], 0.0).then_inc(pool_zero, 1)
                pool.wait_ge(pool_zero, i + 1)
                nc.gpsimd.affine_select(out=m[:], in_=m[:], compare_op=ALU.not_equal, fill=1.0, base=0,
                                        pattern=[[-1, P]], channel_multiplier=1).then_inc(pool_const, 1)
            nc.gpsimd.memset(sel_sum[:], 0.0).then_inc(pool_zero, 1)
            nc.gpsimd.memset(sel_row[:], 0.0).then_inc(pool_zero, 1)
            pool.wait_ge(pool_zero, 5)
            v = sel_sum[:].rearrange("p u (r e) -> p u r e", e=UNITS)
            nc.gpsimd.affine_select(out=v, in_=v, compare_op=ALU.not_equal, fill=WS, base=0,
                                    pattern=[[1, UNITS], [0, HD // UNITS], [-1, UNITS]],
                                    channel_multiplier=0).then_inc(pool_const, 1)
            nc.gpsimd.affine_select(out=sel_row[:], in_=sel_row[:], compare_op=ALU.not_equal, fill=1.0, base=0,
                                    pattern=[[-1, UNITS], [-HD, HC], [0, HD]],
                                    channel_multiplier=1).then_inc(pool_const, 1)

            def carry_waits(cell):
                nc.gpsimd.tensor_tensor(pool_cell[:, cell:cell + 1], pool_cell[:, 0:1], pool_cell[:, 0:1], ALU.add)

            def normalise_x(t, par):
                pool.wait_ge(mv1_ready, G * (t + 1))
                wait(pool, z_ready, G * t)
                carry_waits(1)
                nc.gpsimd.tensor_scalar(negm1[:], mv1[:, :, 0], -1.0, 0.0, ALU.mult, ALU.add).then_inc(norm1, 1)
                nc.gpsimd.tensor_scalar(ve1[:], mv1[:, :, 1], 1.0, EPS, ALU.mult, ALU.add).then_inc(norm1, 1)
                pool.wait_ge(norm1, 3 * t + 2)
                nc.gpsimd.tensor_tensor(rstd1[:], ve1[:], mhalf[:], ALU.pow).then_inc(norm1, 1)
                pool.wait_ge(norm1, 3 * t + 3)
                wait(pool, hhi_ready, G * t)
                wait(pool, hlo_ready, G * t)
                carry_waits(2)
                for b in range(G):
                    nc.gpsimd.tensor_scalar(z_sb[:, b], x_sb[:, par, b], negm1[:, b:b + 1], rstd1[:, b:b + 1],
                                            ALU.add, ALU.mult).then_inc(z_ready, 1)

            def add_beta(g, par):
                pool.wait_ge(y_init, G * (g + 1))
                for b in range(G):
                    nc.gpsimd.tensor_tensor(y_sb[:, par, b], y_sb[:, par, b], beta_sb[:], ALU.add).then_inc(y_beta, 1)

            def add_o(g, par):
                pool.wait_ge(o_ready, G * (g + 1))
                pool.wait_ge(y_beta, G * (g + 1))
                nc.gpsimd.tensor_tensor(y_sb[:, par], y_sb[:, par], o_sb[:], ALU.add).then_inc(y_o, 1)

            def normalise_o(g):
                pool.wait_ge(mv2_ready, G * (g + 1))
                wait(pool, t_ready, G * g)
                carry_waits(3)
                nc.gpsimd.tensor_scalar(negm2[:], mv2[:, :, 0], -1.0, 0.0, ALU.mult, ALU.add).then_inc(norm2, 1)
                nc.gpsimd.tensor_scalar(ve2[:], mv2[:, :, 1], 1.0, EPS, ALU.mult, ALU.add).then_inc(norm2, 1)
                pool.wait_ge(norm2, 4 * g + 2)
                nc.gpsimd.tensor_tensor(rstd2[:], ve2[:], mhalf[:], ALU.pow).then_inc(norm2, 1)
                pool.wait_ge(norm2, 4 * g + 3)
                nc.gpsimd.tensor_tensor(nb2[:], negm2[:], rstd2[:], ALU.mult).then_inc(norm2, 1)

            def finish(g, par, b):
                pool.wait_ge(t_ready, G * g + b + 1)
                nc.gpsimd.tensor_tensor(t_sb[:, b], t_sb[:, b], gamma_sb[:], ALU.mult).then_inc(tg_ready, 1)
                pool.wait_ge(tg_ready, G * g + b + 1)
                pool.wait_ge(y_o, g + 1)
                nc.gpsimd.tensor_tensor(y_sb[:, par, b], y_sb[:, par, b], t_sb[:, b], ALU.add).then_inc(y_ready, 1)

            def step(t, par, a, bc, d, prep):
                if bc:
                    add_beta(t - 1, 1 - par)
                if prep:
                    normalise_x(t + 1, 1 - par)
                if d:
                    normalise_o(t - 2)
                    add_o(t - 2, par)
                    for b in range(G):
                        finish(t - 2, par, b)
                    pool.wait_ge(y_ready, 4 * (t - 1))
                    nc.gpsimd.dma_start(og[t - 2], y_sb[:, par]).then_inc(stored, 16)

            nc.gpsimd.memset(pool_cell[:], 0.0).then_inc(pool_zero, 1)
            pool.wait_ge(pool_zero, 6)
            pool.wait_ge(c_load, 16 * 7)
            pool.wait_ge(dve_const, 1)
            normalise_x(0, 0)
            pipeline(pool, step)
            pool.wait_ge(stored, 16 * STEPS)


DVE_CONST = 22
ACT_CONST = 3

_INS = ["x", "adj", "L0_gnn_b", "L1_gnn_w_qkv", "L1_gnn_w_proj", "L1_gnn_b_proj", "L1_gnn_ln_gamma", "L1_gnn_ln_beta"]


def kernel(**inputs):
    import concourse.bacc as bacc
    from concourse.bass_utils import run_bass_kernel_spmd

    nc = bacc.Bacc("TRN2", target_bir_lowering=False, num_devices=1)
    arrays, args = {}, []
    for name in _INS:
        a = np.ascontiguousarray(inputs[name])
        arrays[f"in_{name}"] = a
        args.append(nc.dram_tensor(f"in_{name}", a.shape, mybir.dt.from_np(a.dtype), kind="ExternalInput").ap())
    out = nc.dram_tensor("out", (B, N, D), mybir.dt.float32, kind="ExternalOutput").ap()
    build(nc, *args, out)
    r = run_bass_kernel_spmd(nc, [arrays], core_ids=[0])
    return r.results[0]["out"]
```

```python
from contextlib import ExitStack

import numpy as np
import concourse.bass as bass
from concourse import mybir

B, N, D = 128, 128, 256
H, HD = 8, 32
G = 4
STEPS = B // G
P = 128
DC = D // P
HC = P // HD
UNITS = G * DC
STACK = 3 * HD
ROWS = STACK + 2
WS = 16.0
MS = 32.0
MASKED = -1e30
SCALE = float(HD) ** -0.5 / (WS * WS)
EPS = 1e-5
SC_SLOTS = 3
SUM_SEL = 2.0 ** -8
ROW_SEL = 2.0 ** -8
OS = WS * ROW_SEL / SUM_SEL
P_SLOTS = 4
PAIRS = 4 * DC * G * N
DMAS = 3 * HC


def build(nc, x, adj, bias0, w_qkv, w_proj, b_proj, gamma, beta, out):
    F32, F16, BF16 = mybir.dt.float32, mybir.dt.float16, mybir.dt.bfloat16
    ALU, ACT, AX = mybir.AluOpType, mybir.ActivationFunctionType, mybir.AxisListType

    with ExitStack() as ctx:
        def sb(name, shape, dt=F32):
            return ctx.enter_context(nc.sbuf_tensor(name, shape, dt))

        def ps(name, shape, dt=F32):
            return ctx.enter_context(nc.psum_tensor(name, shape, dt))

        def sem(name):
            return ctx.enter_context(nc.semaphore(name))

        adj_sb = sb("adj_sb", [P, N])
        w_sb = sb("w_sb", [P, DC, 3 * D])
        wp_sb = sb("wp_sb", [P, DC, D])
        gamma_sb = sb("gamma_sb", [P, D])
        beta_sb = sb("beta_sb", [P, D])
        bproj_sb = sb("bproj_sb", [P, D])
        bproj_r1 = sb("bproj_r1", [P, D])
        bproj_r2 = sb("bproj_r2", [P, D])
        bias0_sb = sb("bias0_sb", [P, 1])
        w_hi = sb("w_hi", [P, DC, 3 * D], F16)
        w_lo = sb("w_lo", [P, DC, 3 * D], F16)
        adjT_hi = sb("adjT_hi", [P, N], F16)
        adjT_lo = sb("adjT_lo", [P, N], F16)
        mask_q = sb("mask_q", [P, HC, N], BF16)
        mask_k = sb("mask_k", [P, HC, N], BF16)
        bp_parts = sb("bp_parts", [P, 3, D], F16)
        bp_rows = sb("bp_rows", [P, D], F16)
        bias_ones = sb("bias_ones", [P, P], F16)
        identf = sb("identf", [P, P])
        ident16 = sb("ident16", [P, P], F16)
        identb = sb("identb", [P, P], BF16)
        sel_sum = sb("sel_sum", [P, UNITS, HD])
        sel_row = sb("sel_row", [P, UNITS, HC, HD], F16)
        lo_pick = sb("lo_pick", [P, HC, UNITS])
        lo_rows = sb("lo_rows", [P, 1])
        wp_hi = sb("wp_hi", [P, DC, D], F16)
        wp_lo = sb("wp_lo", [P, DC, D], F16)
        mhalf = sb("mhalf", [P, G])
        dve_cell = sb("dve_cell", [P, 2])
        pool_cell = sb("pool_cell", [P, 4])
        x_sb = sb("x_sb", [P, 2, G, D])
        y_sb = sb("y_sb", [P, 2, G, D])
        st1 = sb("st1", [P, G, 6])
        mv1 = sb("mv1", [P, G, 2])
        negm1 = sb("negm1", [P, G])
        ve1 = sb("ve1", [P, G])
        rstd1 = sb("rstd1", [P, G])
        z_sb = sb("z_sb", [P, G, D])
        h_hi = sb("h_hi", [P, G, D], F16)
        h_lo = sb("h_lo", [P, G, D], F16)
        hT = sb("hT", [P, 2, DC, G, N], F16)
        amax = sb("amax", [P, G])
        l0 = sb("l0", [P, 2, G])
        v_sb = sb("v_sb", [P, 2, G, D])
        pairs = sb("pairs", [P, 2, DC, 2, G * N], F16)
        stack = sb("stack", [P, 2, 2, H, G, N], F16)
        smax = sb("smax", [P, H, G])
        crow = sb("crow", [H * G, 2, N], F16)
        p_sb = sb("p_sb", [P, P_SLOTS, HC, N])
        pv_sb = sb("pv_sb", [P, G, DC, N])
        rsum = sb("rsum", [P, N])
        rsum16 = sb("rsum16", [P, N], F16)
        rpair = sb("rpair", [P, N], F16)
        oT = sb("oT", [P, G, DC, N])
        oT_hi = sb("oT_hi", [P, G, DC, N], F16)
        oT_lo = sb("oT_lo", [P, G, DC, N], F16)
        o_sb = sb("o_sb", [P, G, D])
        st2 = sb("st2", [P, G, 6])
        mv2 = sb("mv2", [P, G, 2])
        ve2 = sb("ve2", [P, G])
        rstd2 = sb("rstd2", [P, G])
        t_sb = sb("t_sb", [P, G, D])

        sc_ps = [ps(f"sc_ps{i}", [P, HC, N]) for i in range(SC_SLOTS)]
        a_ps = [ps(f"a_ps{i}", [P, G * N]) for i in range(2)]
        sum_ps = ps("sum_ps", [P, 4, N])
        pv_ps = ps("pv_ps", [P, 2 * DC, N])
        o_ps = ps("o_ps", [P, 2, D])

        c_load = sem("c_load")
        pool_const = sem("pool_const")
        act_const = sem("act_const")
        dve_const = sem("dve_const")
        adjT_ps = sem("adjT_ps")
        x_loaded = sem("x_loaded")
        stats1 = sem("stats1")
        mv1_ready = sem("mv1_ready")
        norm1 = sem("norm1")
        z_ready = sem("z_ready")
        hhi_ready = sem("hhi_ready")
        hlo_ready = sem("hlo_ready")
        hT_psum = sem("hT_psum")
        hT_ready = sem("hT_ready")
        a_psum = sem("a_psum")
        amax_ready = sem("amax_ready")
        l0_ready = sem("l0_ready")
        v_psum = sem("v_psum")
        v_ready = sem("v_ready")
        qk_psum = sem("qk_psum")
        qkhi_ready = sem("qkhi_ready")
        qklo_ready = sem("qklo_ready")
        stacked = [sem(f"stacked{j}") for j in range(DC)]
        s_psum = sem("s_psum")
        smax_ready = sem("smax_ready")
        maxT_psum = sem("maxT_psum")
        chi_ready = sem("chi_ready")
        clo_ready = sem("clo_ready")
        crow_in = sem("crow_in")
        st_psum = sem("st_psum")
        p_ready = sem("p_ready")
        pv_psum = sem("pv_psum")
        pv_ready = sem("pv_ready")
        rsum_ready = sem("rsum_ready")
        rsum16_ready = sem("rsum16_ready")
        rpair_ready = sem("rpair_ready")
        r_psum = sem("r_psum")
        oT_ready = sem("oT_ready")
        ohi_ready = sem("ohi_ready")
        olo_ready = sem("olo_ready")
        o_psum = sem("o_psum")
        o_ready = sem("o_ready")
        stats2 = sem("stats2")
        mv2_ready = sem("mv2_ready")
        norm2 = sem("norm2")
        y_init = sem("y_init")
        y_beta = sem("y_beta")
        y_o = sem("y_o")
        tg_ready = sem("tg_ready")
        y_ready = sem("y_ready")
        stored = sem("stored")
        pool_zero = sem("pool_zero")

        xg = x.rearrange("(g b) n d -> g n b d", b=G)
        og = out.rearrange("(g b) n d -> g n b d", b=G)

        def wait(eng, s, value):
            if not isinstance(value, int) or value > 0:
                eng.wait_ge(s, value)

        def pipeline(eng, step):
            step(0, 0, True, False, False, True)
            step(1, 1, True, True, False, True)
            with eng.Fori(2, STEPS - 2, 2) as t:
                step(t, 0, True, True, True, True)
                step(t + 1, 1, True, True, True, True)
            step(STEPS - 2, 0, True, True, True, True)
            step(STEPS - 1, 1, True, True, True, False)
            step(STEPS, 0, False, True, True, False)
            step(STEPS + 1, 1, False, False, True, False)

        block = ctx.enter_context(nc.Block())

        @block.sync
        def _(sp):
            nc.sync.dma_start(x_sb[:, 0], xg[0]).then_inc(x_loaded, 16)
            nc.sync.dma_start(adj_sb[:], adj).then_inc(c_load, 16)
            nc.sync.dma_start(w_sb[:], w_qkv.rearrange("(c p) n -> p c n", p=P)).then_inc(c_load, 16)
            nc.sync.dma_start(wp_sb[:], w_proj.rearrange("(c p) n -> p c n", p=P)).then_inc(c_load, 16)
            nc.sync.dma_start(bias0_sb[:], bias0.rearrange("(p o) -> p o", o=1)).then_inc(c_load, 16)
            for vec, dst in ((gamma, gamma_sb), (beta, beta_sb), (b_proj, bproj_sb)):
                nc.sync.dma_start(dst[:], vec.rearrange("(o d) -> o d", o=1).to_broadcast([P, D])).then_inc(c_load, 16)

            def step(t, par, a, bc, d, prep):
                if bc:
                    for part, done in enumerate((chi_ready, clo_ready)):
                        sp.wait_ge(done, t)
                        row = stack[STACK + part:STACK + part + 1, 1 - par, 0].rearrange("p h b n -> p (h b) n")
                        nc.sync.dma_start(row, crow[:, part]).then_inc(crow_in, 16)
                if a:
                    for j in range(DC):
                        if j == 0:
                            wait(sp, st_psum, UNITS * (t - 1))
                        both = sp.snap(4 * t + 2 * j + 2) if not isinstance(t, int) else 4 * t + 2 * j + 2
                        wait(sp, qkhi_ready, both)
                        wait(sp, qklo_ready, both)
                        for i in range(HC):
                            head = slice(HD * i, HD * (i + 1))
                            high = bass.AP(pairs[:].tensor, HD * i * PAIRS + 2 * j * G * N,
                                           [[PAIRS, HD], [(2 * DC + 1) * G * N, 2], [1, G * N]])
                            for blk, src in enumerate((high, pairs[head, 0, j], pairs[head, 1, j])):
                                dst = stack[blk * HD:(blk + 1) * HD, par, :, HC * j + i]
                                nc.sync.dma_start(dst.rearrange("p s b n -> p s (b n)"), src).then_inc(stacked[j], 16)

            pipeline(sp, step)

        @block.tensor
        def _(pe):
            pe.wait_ge(c_load, 16 * 7)
            pe.wait_ge(pool_const, 1)
            nc.tensor.transpose(sc_ps[0][:, 0, :], adj_sb[:], identf[:]).then_inc(adjT_ps, 1)
            pe.wait_ge(pool_const, 7)
            pe.wait_ge(dve_const, DVE_CONST)
            pe.wait_ge(act_const, ACT_CONST)

            def transpose_h(t, b):
                pe.wait_ge(hhi_ready, 4 * t + b + 1)
                pe.wait_ge(hlo_ready, 4 * t + b + 1)
                if b < 2:
                    wait(pe, v_ready, 2 * t - 1 + b)
                else:
                    pe.wait_ge(hT_ready, 4 * t + b - 1)
                to = a_ps[b % 2][:].bitcast(F16)
                for i, (h, c) in enumerate(((h_hi, 0), (h_hi, 1), (h_lo, 0), (h_lo, 1))):
                    mm = nc.tensor.transpose(to[:, i * N:(i + 1) * N], h[:, b, c * P:(c + 1) * P], ident16[:])
                mm.then_inc(hT_psum, 1)

            def layer0(t, i):
                pe.wait_ge(qkhi_ready, 4 * t + i + 1)
                pe.wait_ge(qklo_ready, 4 * t + i + 1)
                for k, (w, h) in enumerate(((adjT_hi, h_hi), (adjT_hi, h_lo), (adjT_lo, h_hi))):
                    mm = nc.tensor.matmul(a_ps[i][:], w[:], h[:, 2 * i:2 * i + 2].rearrange("p b d -> p (b d)"),
                                          start=(k == 0), stop=(k == 2))
                mm.then_inc(a_psum, 1)

            def project_qk(t, c):
                if c == 0:
                    pe.wait_ge(hT_ready, 4 * t + 4)
                if c >= 2:
                    pe.wait_ge(amax_ready, 2 * t + c - 1)
                col = (c % 2) * D + (c // 2) * P
                k = 0
                for w, part in ((w_hi, 0), (w_hi, 1), (w_lo, 0)):
                    for dc in range(DC):
                        mm = nc.tensor.matmul(a_ps[c % 2][:], w[:, dc, col:col + P],
                                              hT[:, part, dc].rearrange("p b n -> p (b n)"),
                                              start=(k == 0), stop=(k == 5))
                        k += 1
                mm.then_inc(qk_psum, 1)

            def project_v(t, i):
                pe.wait_ge(qkhi_ready, 4 * t + 3 + i)
                pe.wait_ge(qklo_ready, 4 * t + 3 + i)
                for bb in range(2):
                    k = 0
                    for part, w in ((0, w_hi), (1, w_hi), (0, w_lo)):
                        for dc in range(DC):
                            mm = nc.tensor.matmul(a_ps[i][:, bb * D:(bb + 1) * D], hT[:, part, dc, 2 * i + bb],
                                                  w[:, dc, 2 * D:3 * D], start=(k == 0), stop=(k == 5))
                            k += 1
                mm.then_inc(v_psum, 1)

            def scores(g, par, u):
                j, b = u // G, u % G
                if b == 0:
                    pe.wait_ge(stacked[j], 16 * DMAS * (g + 1))
                if u < SC_SLOTS:
                    wait(pe, p_ready, UNITS * (g - 1) + (8, 6, 7)[u])
                else:
                    pe.wait_ge(smax_ready, UNITS * g + u - SC_SLOTS + 1)
                to = sc_ps[u % SC_SLOTS]
                nc.tensor.matmul(to[:].rearrange("p h n -> p (h n)"), identb[:],
                                 mask_q[:].rearrange("p h n -> p (h n)"), start=True, stop=False, skip_group_check=True)
                for i in range(HC):
                    h = HC * j + i
                    mm = nc.tensor.matmul(to[:, i], stack[0:STACK, par, 0, h, b], stack[0:STACK, par, 1, h, b],
                                          start=False, stop=True, skip_group_check=True)
                mm.then_inc(s_psum, 1)

            def transpose_max(g):
                pe.wait_ge(smax_ready, UNITS * (g + 1))
                wait(pe, rsum_ready, g)
                nc.tensor.transpose(sum_ps[0:H * G, 1, :], smax[:].rearrange("p h b -> p (h b)"),
                                    identf[:]).then_inc(maxT_psum, 1)

            def scores_T(g, par, u):
                b, j = u // DC, u % DC
                if u == 0:
                    pe.wait_ge(crow_in, 32 * (g + 1))
                if u < SC_SLOTS:
                    pe.wait_ge(smax_ready, UNITS * g + 6 + u)
                else:
                    pe.wait_ge(p_ready, UNITS * g + u - SC_SLOTS + 1)
                to = sc_ps[(UNITS + u) % SC_SLOTS]
                nc.tensor.matmul(to[:].rearrange("p h n -> p (h n)"), identb[:],
                                 mask_k[:].rearrange("p h n -> p (h n)"), start=True, stop=False, skip_group_check=True)
                for i in range(HC):
                    h = HC * j + i
                    mm = nc.tensor.matmul(to[:, i], stack[0:ROWS, par, 1, h, b], stack[0:ROWS, par, 0, h, b],
                                          start=False, stop=True, skip_group_check=True)
                mm.then_inc(st_psum, 1)

            def values(g, par, u):
                b, j = u // DC, u % DC
                pe.wait_ge(p_ready, UNITS * g + u + 1)
                if j == 0:
                    if b % 2 == 0:
                        pe.wait_ge(v_ready, 2 * g + b // 2 + 1)
                    wait(pe, pv_ready, G * g + b)
                if u == 0:
                    wait(pe, oT_ready, G * g)
                    wait(pe, rsum_ready, g)
                    pe.wait_ge(clo_ready, g + 1)
                for i in range(HC):
                    h = HC * j + i
                    nc.tensor.matmul(pv_ps[HD * i:HD * (i + 1), j], v_sb[:, par, b, HD * h:HD * (h + 1)],
                                     p_sb[:, u % P_SLOTS, i], start=True, stop=True)
                for i in range(HC):
                    mm = nc.tensor.matmul(sum_ps[HD * i:HD * (i + 1), 0], sel_sum[:, u], p_sb[:, u % P_SLOTS, i],
                                          start=(u == 0), stop=(u == UNITS - 1), skip_group_check=True)
                mm.then_inc(pv_psum, 1)

            def spread(g, b):
                if b == 0:
                    pe.wait_ge(rpair_ready, g + 1)
                    pe.wait_ge(pv_ready, G * (g + 1))
                else:
                    pe.wait_ge(oT_ready, G * g + b)
                for j in range(DC):
                    mm = nc.tensor.matmul(pv_ps[:, j], sel_row[:, b * DC + j].rearrange("p h d -> p (h d)"), rpair[:],
                                          start=True, stop=True)
                mm.then_inc(r_psum, 1)

            def project_o(g, b):
                pe.wait_ge(ohi_ready, G * g + b + 1)
                pe.wait_ge(olo_ready, G * g + b + 1)
                wait(pe, o_ready, G * g + b)
                nc.tensor.matmul(o_ps[:, 0], bias_ones[:], bp_rows[:], start=True, stop=False)
                for k, (o, w) in enumerate(((oT_hi, wp_hi), (oT_hi, wp_lo), (oT_lo, wp_hi))):
                    for j in range(DC):
                        mm = nc.tensor.matmul(o_ps[:, 0], o[:, b, j], w[:, j], start=False, stop=(k == 2 and j == DC - 1))
                mm.then_inc(o_psum, 1)

            ORDER = ("S0 T0 S1 T1 S2 T2 R0 S3 T3 R1 S4 O0 S5 R2 S6 O1 S7 R3 Q0 O2 M0 Q1 O3 "
                     "L0 L1 E0 E1 Q2 E2 P0 P1 Q3 E3 P2 E4 P3 V0 E5 P4 E6 P5 E7 V1 P6 P7").split()

            def step(t, par, a, bc, d, prep):
                for what in ORDER:
                    kind, i = what[0], int(what[1])
                    if kind == "T" and a:
                        transpose_h(t, i)
                    elif kind == "L" and a:
                        layer0(t, i)
                    elif kind == "Q" and a:
                        project_qk(t, i)
                    elif kind == "V" and a:
                        project_v(t, i)
                    elif kind == "S" and bc:
                        scores(t - 1, 1 - par, i)
                    elif kind == "M" and bc:
                        transpose_max(t - 1)
                    elif kind == "E" and bc:
                        scores_T(t - 1, 1 - par, i)
                    elif kind == "P" and bc:
                        values(t - 1, 1 - par, i)
                    elif kind == "R" and d:
                        spread(t - 2, i)
                    elif kind == "O" and d:
                        project_o(t - 2, i)

            pipeline(pe, step)

        @block.scalar
        def _(act):
            act.wait_ge(c_load, 16 * 7)
            nc.scalar.activation(w_hi[:], w_sb[:], ACT.Copy, scale=WS).then_inc(act_const, 1)
            nc.scalar.activation(bp_parts[:, 0], bproj_sb[:], ACT.Copy).then_inc(act_const, 1)
            nc.scalar.activation(wp_hi[:], wp_sb[:], ACT.Copy, scale=WS).then_inc(act_const, 1)
            act.wait_ge(adjT_ps, 1)
            nc.scalar.activation(adjT_hi[:], sc_ps[0][:, 0, :], ACT.Copy, scale=WS).then_inc(act_const, 1)

            def h_high(t, b):
                act.wait_ge(z_ready, G * t + b + 1)
                if b == 0:
                    wait(act, a_psum, 2 * t)
                    wait(act, hT_psum, G * t)
                nc.scalar.activation(h_hi[:, b], z_sb[:, b], ACT.Relu).then_inc(hhi_ready, 1)

            def take_hT(t, b):
                act.wait_ge(hT_psum, G * t + b + 1)
                if b == 0:
                    wait(act, v_psum, 2 * t)
                nc.scalar.activation(hT[:, :, :, b, :],
                                     a_ps[b % 2][:].bitcast(F16)[:, 0:4 * N].rearrange("p (s c n) -> p s c n", s=2, c=DC),
                                     ACT.Copy).then_inc(hT_ready, 1)

            def layer0_numbers(t, par):
                act.wait_ge(amax_ready, 2 * (t + 1))
                nc.scalar.activation(l0[:, par], amax[:], ACT.Relu, bias=bias0_sb[:, 0:1],
                                     scale=1.0 / WS).then_inc(l0_ready, 1)

            def start_y(g, par, b):
                if b == 0:
                    act.wait_ge(l0_ready, g + 1)
                    wait(act, stored, 16 * (g - 1))
                nc.scalar.activation(y_sb[:, par, b], x_sb[:, par, b], ACT.Identity,
                                     bias=l0[:, par, b:b + 1]).then_inc(y_init, 1)

            def load_x(t, par):
                wait(act, y_init, G * (t - 1))
                nc.scalar.dma_start(x_sb[:, par], xg[t]).then_inc(x_loaded, 16)

            def take_v(t, par, i):
                act.wait_ge(v_psum, 2 * t + i + 1)
                nc.scalar.activation(v_sb[:, par, 2 * i:2 * i + 2].rearrange("p b d -> p (b d)"), a_ps[i][:],
                                     ACT.Copy).then_inc(v_ready, 1)

            def qk_high(t, c):
                act.wait_ge(qk_psum, 4 * t + c + 1)
                if c % 2 == 0:
                    wait(act, stacked[c // 2], 16 * DMAS * t)
                nc.scalar.activation(pairs[:, c % 2, c // 2, c % 2], a_ps[c % 2][:], ACT.Copy).then_inc(qkhi_ready, 1)

            def max_high(g):
                act.wait_ge(maxT_psum, g + 1)
                wait(act, crow_in, 32 * g)
                nc.scalar.activation(crow[:, 0], sum_ps[0:H * G, 1, :], ACT.Copy, scale=-1.0 / MS).then_inc(chi_ready, 1)

            def exps(g, u):
                act.wait_ge(st_psum, UNITS * g + u + 1)
                wait(act, pv_psum, UNITS * g + u - P_SLOTS + 1)
                nc.scalar.activation(p_sb[:, u % P_SLOTS], sc_ps[(UNITS + u) % SC_SLOTS][:], ACT.Exp,
                                     scale=SCALE).then_inc(p_ready, 1)

            def take_pv(g, b):
                act.wait_ge(pv_psum, UNITS * g + DC * (b + 1))
                if b == 0:
                    wait(act, oT_ready, G * g)
                nc.scalar.activation(pv_sb[:, b], pv_ps[:, 0:DC], ACT.Copy).then_inc(pv_ready, 1)

            def o_high(g, b):
                act.wait_ge(oT_ready, G * g + b + 1)
                if b == 0:
                    wait(act, o_psum, G * g)
                nc.scalar.activation(oT_hi[:, b], oT[:, b], ACT.Copy).then_inc(ohi_ready, 1)

            def take_o(g, b):
                act.wait_ge(o_psum, G * g + b + 1)
                if b == 0:
                    wait(act, y_o, G * g)
                    wait(act, tg_ready, G * g)
                nc.scalar.activation(o_sb[:, b], o_ps[:, 0], ACT.Copy, scale=1.0 / (OS * WS)).then_inc(o_ready, 1)

            ORDER = ("T0 T1 T2 C0 T3 C1 O0 C2 O1 Y0 C3 Y1 Q0 O2 Y2 M0 Q1 Y3 X0 O3 L0 "
                     "E0 E1 Q2 E2 A0 Q3 E3 H0 E4 A1 H1 V0 E5 H2 E6 A2 H3 E7 V1 A3").split()

            def step(t, par, a, bc, d, prep):
                for what in ORDER:
                    kind, i = what[0], int(what[1])
                    if kind == "Y" and bc:
                        start_y(t - 1, 1 - par, i)
                    elif kind == "T" and a:
                        take_hT(t, i)
                    elif kind == "L" and a:
                        layer0_numbers(t, par)
                    elif kind == "Q" and a:
                        qk_high(t, i)
                    elif kind == "V" and a:
                        take_v(t, par, i)
                    elif kind == "M" and bc:
                        max_high(t - 1)
                    elif kind == "E" and bc:
                        exps(t - 1, i)
                    elif kind == "A" and bc:
                        take_pv(t - 1, i)
                    elif kind == "O" and d:
                        take_o(t - 2, i)
                    elif kind == "C" and d:
                        o_high(t - 2, i)
                    elif kind == "X" and prep:
                        load_x(t + 1, 1 - par)
                    elif kind == "H" and prep:
                        h_high(t + 1, i)

            for b in range(G):
                h_high(0, b)
            pipeline(act, step)

        @block.vector
        def _(dve):
            nc.vector.memset(mhalf[:], -0.5).then_inc(dve_const, 1)
            nc.vector.memset(bias_ones[:], OS * WS).then_inc(dve_const, 1)
            nc.vector.memset(bp_rows[:], 0.0).then_inc(dve_const, 1)
            for par in range(2):
                nc.vector.memset(stack[STACK:ROWS, par, 1], MS).then_inc(dve_const, 1)
            dve.wait_ge(c_load, 16 * 7)
            for i in range(HC):
                nc.vector.tensor_scalar(mask_q[:, i], adj_sb[:], 0.0, MASKED, ALU.is_equal, ALU.mult).then_inc(dve_const, 1)
            dve.wait_ge(act_const, 4)
            dve.wait_ge(adjT_ps, 1)
            for i in range(HC):
                nc.vector.tensor_scalar(mask_k[:, i], sc_ps[0][:, 0, :], 0.0, MASKED, ALU.is_equal, ALU.mult).then_inc(dve_const, 1)
            nc.vector.scalar_tensor_tensor(adjT_lo[:], sc_ps[0][:, 0, :], WS, adjT_hi[:], ALU.mult, ALU.subtract).then_inc(dve_const, 1)
            nc.vector.scalar_tensor_tensor(w_lo[:], w_sb[:], WS, w_hi[:], ALU.mult, ALU.subtract).then_inc(dve_const, 1)
            nc.vector.scalar_tensor_tensor(wp_lo[:], wp_sb[:], WS, wp_hi[:], ALU.mult, ALU.subtract).then_inc(dve_const, 1)
            dve.wait_ge(pool_const, 7)
            nc.vector.tensor_reduce(lo_rows[:], lo_pick[:].rearrange("p h u -> p (h u)"), AX.X, ALU.add).then_inc(dve_const, 1)
            nc.vector.tensor_tensor(bproj_r1[:], bproj_sb[:], bp_parts[:, 0], ALU.subtract).then_inc(dve_const, 1)
            dve.wait_ge(dve_const, 18)
            nc.vector.tensor_copy(bp_parts[:, 1], bproj_r1[:]).then_inc(dve_const, 1)
            dve.wait_ge(dve_const, 19)
            nc.vector.tensor_tensor(bproj_r2[:], bproj_r1[:], bp_parts[:, 1], ALU.subtract).then_inc(dve_const, 1)
            dve.wait_ge(dve_const, 20)
            nc.vector.tensor_copy(bp_parts[:, 2], bproj_r2[:]).then_inc(dve_const, 1)
            dve.wait_ge(dve_const, 21)
            for i in range(3):
                nc.vector.tensor_copy(bp_rows[HD * i:HD * i + 1], bp_parts[HD * i:HD * i + 1, i]).then_inc(dve_const, 1)

            def stats_x(t, par):
                dve.wait_ge(x_loaded, 16 * (t + 1))
                wait(dve, mv1_ready, G * t)
                for b in range(G):
                    nc.vector.bn_stats(st1[:, b], x_sb[:, par, b]).then_inc(stats1, 1)
                dve.wait_ge(stats1, G * (t + 1))
                wait(dve, norm1, 3 * t)
                nc.vector.memset(dve_cell[:, 0:1], 0.0)
                for b in range(G):
                    nc.vector.bn_aggr(mv1[:, b], st1[:, b]).then_inc(mv1_ready, 1)

            def h_low(t, b):
                dve.wait_ge(hhi_ready, G * t + b + 1)
                if b == 0:
                    wait(dve, a_psum, 2 * t)
                nc.vector.scalar_tensor_tensor(h_lo[:, b], z_sb[:, b], 0.0, h_hi[:, b], ALU.max,
                                               ALU.subtract).then_inc(hlo_ready, 1)

            def layer0_max(t, i):
                dve.wait_ge(a_psum, 2 * t + i + 1)
                if i == 0:
                    wait(dve, l0_ready, t)
                nc.vector.tensor_reduce(amax[:, 2 * i:2 * i + 2], a_ps[i][:].rearrange("p (b d) -> p b d", b=2), AX.X,
                                        ALU.max).then_inc(amax_ready, 1)

            def qk_low(t, c):
                dve.wait_ge(qkhi_ready, 4 * t + c + 1)
                if c % 2 == 0:
                    wait(dve, stacked[c // 2], 16 * DMAS * t)
                nc.vector.tensor_tensor(pairs[:, 1 - c % 2, c // 2, c % 2], a_ps[c % 2][:], pairs[:, c % 2, c // 2, c % 2],
                                        ALU.subtract).then_inc(qklo_ready, 1)

            def row_max(g, u):
                j, b = u // G, u % G
                dve.wait_ge(s_psum, UNITS * g + u + 1)
                if u == 0:
                    wait(dve, maxT_psum, g)
                nc.vector.tensor_reduce(smax[:, HC * j:HC * (j + 1), b], sc_ps[u % SC_SLOTS][:], AX.X,
                                        ALU.max).then_inc(smax_ready, 1)

            def max_low(g):
                dve.wait_ge(chi_ready, g + 1)
                wait(dve, crow_in, 32 * g)
                nc.vector.scalar_tensor_tensor(crow[:, 1], sum_ps[0:H * G, 1, :], -1.0 / MS, crow[:, 0], ALU.mult,
                                               ALU.subtract).then_inc(clo_ready, 1)

            def invert_sums(g):
                dve.wait_ge(pv_psum, UNITS * (g + 1))
                nc.vector.reciprocal(rsum[:], sum_ps[:, 0, :]).then_inc(rsum_ready, 1)
                dve.wait_ge(rsum_ready, g + 1)
                nc.vector.tensor_copy(rsum16[:], rsum[:]).then_inc(rsum16_ready, 1)
                dve.wait_ge(rsum16_ready, g + 1)
                wait(dve, r_psum, G * g)
                nc.vector.scalar_tensor_tensor(rpair[:], rsum16[:], lo_rows[:, 0:1], rsum[:], ALU.mult,
                                               ALU.add).then_inc(rpair_ready, 1)

            def scale_o(g, b):
                dve.wait_ge(r_psum, G * g + b + 1)
                dve.wait_ge(pv_ready, G * g + b + 1)
                if b == 0:
                    wait(dve, ohi_ready, G * g)
                    wait(dve, olo_ready, G * g)
                nc.vector.tensor_tensor(oT[:, b], pv_ps[:, 0:DC], pv_sb[:, b], ALU.mult).then_inc(oT_ready, 1)

            def o_low(g, b):
                dve.wait_ge(ohi_ready, G * g + b + 1)
                if b == 0:
                    wait(dve, o_psum, G * g)
                nc.vector.tensor_tensor(oT_lo[:, b], oT[:, b], oT_hi[:, b], ALU.subtract).then_inc(olo_ready, 1)

            def stats_o(g, b):
                dve.wait_ge(o_ready, G * g + b + 1)
                nc.vector.bn_stats(st2[:, b], o_sb[:, b]).then_inc(stats2, 1)

            def aggregate_o(g):
                dve.wait_ge(stats2, G * (g + 1))
                wait(dve, norm2, 2 * g)
                wait(dve, tg_ready, G * g)
                nc.vector.memset(dve_cell[:, 1:2], 0.0)
                for b in range(G):
                    nc.vector.bn_aggr(mv2[:, b], st2[:, b]).then_inc(mv2_ready, 1)

            def finish(g, par, i):
                if i == 0:
                    dve.wait_ge(norm2, 2 * (g + 1))
                    dve.wait_ge(mv2_ready, G * (g + 1))
                    wait(dve, y_ready, G * g)
                for b in (2 * i, 2 * i + 1):
                    nc.vector.scalar_tensor_tensor(t_sb[:, b], o_sb[:, b], mv2[:, b, 0:1], gamma_sb[:], ALU.subtract,
                                                   ALU.mult).then_inc(tg_ready, 1)
                for b in (2 * i, 2 * i + 1):
                    dve.wait_ge(tg_ready, G * g + b + 1)
                    dve.wait_ge(y_o, G * g + b + 1)
                    nc.vector.scalar_tensor_tensor(y_sb[:, par, b], t_sb[:, b], rstd2[:, b:b + 1], y_sb[:, par, b],
                                                   ALU.mult, ALU.add).then_inc(y_ready, 1)

            ORDER = ("I0 S0 S1 S2 O0 S3 C0 O1 S4 C1 S5 O2 B0 S6 C2 O3 S7 C3 B1 "
                     "M0 Q0 B2 Q1 L0 L1 X0 Q2 B3 G0 Q3 H0 H1 H2 F0 H3 F1").split()

            def step(t, par, a, bc, d, prep):
                for what in ORDER:
                    kind, i = what[0], int(what[1])
                    if kind == "I" and d:
                        invert_sums(t - 2)
                    elif kind == "O" and d:
                        scale_o(t - 2, i)
                    elif kind == "C" and d:
                        o_low(t - 2, i)
                    elif kind == "B" and d:
                        stats_o(t - 2, i)
                    elif kind == "G" and d:
                        aggregate_o(t - 2)
                    elif kind == "F" and d:
                        finish(t - 2, par, i)
                    elif kind == "S" and bc:
                        row_max(t - 1, i)
                    elif kind == "M" and bc:
                        max_low(t - 1)
                    elif kind == "L" and a:
                        layer0_max(t, i)
                    elif kind == "Q" and a:
                        qk_low(t, i)
                    elif kind == "X" and prep:
                        stats_x(t + 1, 1 - par)
                    elif kind == "H" and prep:
                        h_low(t + 1, i)

            stats_x(0, 0)
            for b in range(G):
                h_low(0, b)
            pipeline(dve, step)

        @block.gpsimd
        def _(pool):
            for i, m in enumerate((identf, ident16, identb)):
                nc.gpsimd.memset(m[:], 0.0).then_inc(pool_zero, 1)
                pool.wait_ge(pool_zero, i + 1)
                nc.gpsimd.affine_select(out=m[:], in_=m[:], compare_op=ALU.not_equal, fill=1.0, base=0,
                                        pattern=[[-1, P]], channel_multiplier=1).then_inc(pool_const, 1)
            nc.gpsimd.memset(sel_sum[:], 0.0).then_inc(pool_zero, 1)
            nc.gpsimd.memset(sel_row[:], 0.0).then_inc(pool_zero, 1)
            nc.gpsimd.memset(lo_pick[:], 0.0).then_inc(pool_zero, 1)
            pool.wait_ge(pool_zero, 6)
            v = sel_sum[:].rearrange("p u (r e) -> p u r e", e=UNITS)
            nc.gpsimd.affine_select(out=v, in_=v, compare_op=ALU.not_equal, fill=SUM_SEL, base=0,
                                    pattern=[[1, UNITS], [0, HD // UNITS], [-1, UNITS]],
                                    channel_multiplier=0).then_inc(pool_const, 1)
            for part in range(2):
                nc.gpsimd.affine_select(out=sel_row[:], in_=sel_row[:], compare_op=ALU.not_equal, fill=ROW_SEL,
                                        base=-UNITS * part, pattern=[[-1, UNITS], [-HD, HC], [0, HD]],
                                        channel_multiplier=1).then_inc(pool_const, 1)
                pool.wait_ge(pool_const, 5 + part)
            nc.gpsimd.affine_select(out=lo_pick[:], in_=lo_pick[:], compare_op=ALU.not_equal, fill=-1.0, base=-UNITS,
                                    pattern=[[-HD, HC], [-1, UNITS]], channel_multiplier=1).then_inc(pool_const, 1)

            def carry_waits(cell):
                nc.gpsimd.tensor_tensor(pool_cell[:, cell:cell + 1], pool_cell[:, 0:1], pool_cell[:, 0:1], ALU.add)

            def normalise_x(t, par):
                pool.wait_ge(mv1_ready, G * (t + 1))
                wait(pool, z_ready, G * t)
                carry_waits(1)
                nc.gpsimd.tensor_scalar(negm1[:], mv1[:, :, 0], -1.0, 0.0, ALU.mult, ALU.add).then_inc(norm1, 1)
                nc.gpsimd.tensor_scalar(ve1[:], mv1[:, :, 1], 1.0, EPS, ALU.mult, ALU.add).then_inc(norm1, 1)
                pool.wait_ge(norm1, 3 * t + 2)
                nc.gpsimd.tensor_tensor(rstd1[:], ve1[:], mhalf[:], ALU.pow).then_inc(norm1, 1)
                pool.wait_ge(norm1, 3 * t + 3)
                wait(pool, hhi_ready, G * t)
                wait(pool, hlo_ready, G * t)
                carry_waits(2)
                for b in range(G):
                    nc.gpsimd.tensor_scalar(z_sb[:, b], x_sb[:, par, b], negm1[:, b:b + 1], rstd1[:, b:b + 1],
                                            ALU.add, ALU.mult).then_inc(z_ready, 1)

            def add_beta(g, par):
                pool.wait_ge(y_init, G * (g + 1))
                for b in range(G):
                    nc.gpsimd.tensor_tensor(y_sb[:, par, b], y_sb[:, par, b], beta_sb[:], ALU.add).then_inc(y_beta, 1)

            def add_o(g, par, b):
                pool.wait_ge(o_ready, G * g + b + 1)
                if b == 0:
                    pool.wait_ge(y_beta, G * (g + 1))
                nc.gpsimd.tensor_tensor(y_sb[:, par, b], y_sb[:, par, b], o_sb[:, b], ALU.add).then_inc(y_o, 1)

            def normalise_o(g):
                pool.wait_ge(mv2_ready, G * (g + 1))
                wait(pool, y_ready, G * g)
                carry_waits(3)
                nc.gpsimd.tensor_scalar(ve2[:], mv2[:, :, 1], 1.0, EPS, ALU.mult, ALU.add).then_inc(norm2, 1)
                pool.wait_ge(norm2, 2 * g + 1)
                nc.gpsimd.tensor_tensor(rstd2[:], ve2[:], mhalf[:], ALU.pow).then_inc(norm2, 1)

            def step(t, par, a, bc, d, prep):
                if d:
                    for b in range(G - 1):
                        add_o(t - 2, par, b)
                if bc:
                    add_beta(t - 1, 1 - par)
                if d:
                    add_o(t - 2, par, G - 1)
                if prep:
                    normalise_x(t + 1, 1 - par)
                if d:
                    normalise_o(t - 2)
                    pool.wait_ge(y_ready, G * (t - 1))
                    nc.gpsimd.dma_start(og[t - 2], y_sb[:, par]).then_inc(stored, 16)

            nc.gpsimd.memset(pool_cell[:], 0.0).then_inc(pool_zero, 1)
            pool.wait_ge(pool_zero, 7)
            pool.wait_ge(c_load, 16 * 7)
            pool.wait_ge(dve_const, 1)
            normalise_x(0, 0)
            pipeline(pool, step)
            pool.wait_ge(stored, 16 * STEPS)


DVE_CONST = 24
ACT_CONST = 4

_INS = ["x", "adj", "L0_gnn_b", "L1_gnn_w_qkv", "L1_gnn_w_proj", "L1_gnn_b_proj", "L1_gnn_ln_gamma", "L1_gnn_ln_beta"]


def kernel(**inputs):
    import concourse.bacc as bacc
    from concourse.bass_utils import run_bass_kernel_spmd

    nc = bacc.Bacc("TRN2", target_bir_lowering=False, num_devices=1)
    arrays, args = {}, []
    for name in _INS:
        a = np.ascontiguousarray(inputs[name])
        arrays[f"in_{name}"] = a
        args.append(nc.dram_tensor(f"in_{name}", a.shape, mybir.dt.from_np(a.dtype), kind="ExternalInput").ap())
    out = nc.dram_tensor("out", (B, N, D), mybir.dt.float32, kind="ExternalOutput").ap()
    build(nc, *args, out)
    r = run_bass_kernel_spmd(nc, [arrays], core_ids=[0])
    return r.results[0]["out"]
```

```python
from contextlib import ExitStack

import numpy as np
import concourse.bass as bass
from concourse import mybir

B, N, D = 128, 128, 256
H, HD = 8, 32
G = 4
STEPS = B // G
P = 128
DC = D // P
HC = P // HD
UNITS = G * DC
STACK = 3 * HD
ROWS = STACK + 2
WS = 16.0
MS = 32.0
MASKED = -1e30
SCALE = float(HD) ** -0.5 / (WS * WS)
EPS = 1e-5
SC_SLOTS = 3
SUM_SEL = 2.0 ** -8
ROW_SEL = 2.0 ** -8
OS = WS * ROW_SEL / SUM_SEL
P_SLOTS = 4
PAIRS = 4 * DC * G * N
DMAS = 3 * HC
ACT_CONST = 4
DVE_CONST = 14 + 2 * HC


def build(nc, x, adj, bias0, w_qkv, w_proj, b_proj, gamma, beta, out):
    F32, F16, BF16 = mybir.dt.float32, mybir.dt.float16, mybir.dt.bfloat16
    ALU, ACT, AX = mybir.AluOpType, mybir.ActivationFunctionType, mybir.AxisListType

    with ExitStack() as ctx:
        def sb(name, shape, dt=F32):
            return ctx.enter_context(nc.sbuf_tensor(name, shape, dt))

        def ps(name, shape, dt=F32):
            return ctx.enter_context(nc.psum_tensor(name, shape, dt))

        def sem(name):
            return ctx.enter_context(nc.semaphore(name))

        adj_sb = sb("adj_sb", [P, N])
        w_sb = sb("w_sb", [P, DC, 3 * D])
        wp_sb = sb("wp_sb", [P, DC, D])
        gamma_sb = sb("gamma_sb", [P, D])
        beta_sb = sb("beta_sb", [P, D])
        bproj_sb = sb("bproj_sb", [P, D])
        bproj_r1 = sb("bproj_r1", [P, D])
        bproj_r2 = sb("bproj_r2", [P, D])
        bias0_sb = sb("bias0_sb", [P, 1])
        w_hi = sb("w_hi", [P, DC, 3 * D], F16)
        w_lo = sb("w_lo", [P, DC, 3 * D], F16)
        adjT_hi = sb("adjT_hi", [P, N], F16)
        adjT_lo = sb("adjT_lo", [P, N], F16)
        mask_q = sb("mask_q", [P, HC, N], BF16)
        mask_k = sb("mask_k", [P, HC, N], BF16)
        bp_parts = sb("bp_parts", [P, 3, D], F16)
        bp_rows = sb("bp_rows", [P, D], F16)
        bias_ones = sb("bias_ones", [P, P], F16)
        identf = sb("identf", [P, P])
        ident16 = sb("ident16", [P, P], F16)
        identb = sb("identb", [P, P], BF16)
        sel_sum = sb("sel_sum", [P, UNITS, HD])
        sel_row = sb("sel_row", [P, UNITS, HC, HD], F16)
        lo_pick = sb("lo_pick", [P, HC, UNITS])
        lo_rows = sb("lo_rows", [P, 1])
        wp_hi = sb("wp_hi", [P, DC, D], F16)
        wp_lo = sb("wp_lo", [P, DC, D], F16)
        mhalf = sb("mhalf", [P, G])
        dve_cell = sb("dve_cell", [P, 2])
        pool_cell = sb("pool_cell", [P, 4])
        x_sb = sb("x_sb", [P, 2, G, D])
        y_sb = sb("y_sb", [P, 2, G, D])
        st1 = sb("st1", [P, G, 6])
        mv1 = sb("mv1", [P, G, 2])
        negm1 = sb("negm1", [P, G])
        ve1 = sb("ve1", [P, G])
        rstd1 = sb("rstd1", [P, G])
        z_sb = sb("z_sb", [P, G, D])
        h_hi = sb("h_hi", [P, G, D], F16)
        h_lo = sb("h_lo", [P, G, D], F16)
        hT = sb("hT", [P, 2, DC, G, N], F16)
        amax = sb("amax", [P, G])
        l0 = sb("l0", [P, 2, G])
        v_sb = sb("v_sb", [P, 2, G, D])
        pairs = sb("pairs", [P, 2, DC, 2, G * N], F16)
        stack = sb("stack", [P, 2, 2, H, G, N], F16)
        smax = sb("smax", [P, H, G])
        crow = sb("crow", [H * G, 2, N], F16)
        p_sb = sb("p_sb", [P, P_SLOTS, HC, N])
        pv_sb = sb("pv_sb", [P, G, DC, N])
        rsum = sb("rsum", [P, N])
        rsum16 = sb("rsum16", [P, N], F16)
        rpair = sb("rpair", [P, N], F16)
        oT = sb("oT", [P, G, DC, N])
        oT_hi = sb("oT_hi", [P, G, DC, N], F16)
        oT_lo = sb("oT_lo", [P, G, DC, N], F16)
        o_sb = sb("o_sb", [P, G, D])
        st2 = sb("st2", [P, G, 6])
        mv2 = sb("mv2", [P, G, 2])
        ve2 = sb("ve2", [P, G])
        rstd2 = sb("rstd2", [P, G])
        t_sb = sb("t_sb", [P, G, D])

        sc_ps = [ps(f"sc_ps{i}", [P, HC, N]) for i in range(SC_SLOTS)]
        a_ps = [ps(f"a_ps{i}", [P, G * N]) for i in range(2)]
        sum_ps = ps("sum_ps", [P, 4, N])
        pv_ps = ps("pv_ps", [P, 2 * DC, N])
        o_ps = ps("o_ps", [P, 2, D])

        core_load = sem("core_load")
        c_load = sem("c_load")
        pool_const = sem("pool_const")
        act_const = sem("act_const")
        dve_const = sem("dve_const")
        adjT_ps = sem("adjT_ps")
        x_loaded = sem("x_loaded")
        stats1 = sem("stats1")
        mv1_ready = sem("mv1_ready")
        norm1 = sem("norm1")
        z_ready = sem("z_ready")
        hhi_ready = sem("hhi_ready")
        hlo_ready = sem("hlo_ready")
        hT_psum = sem("hT_psum")
        hT_ready = sem("hT_ready")
        a_psum = sem("a_psum")
        amax_ready = sem("amax_ready")
        l0_ready = sem("l0_ready")
        v_psum = sem("v_psum")
        v_ready = sem("v_ready")
        qk_psum = sem("qk_psum")
        qkhi_ready = sem("qkhi_ready")
        qklo_ready = sem("qklo_ready")
        stacked = [sem(f"stacked{j}") for j in range(DC)]
        s_psum = sem("s_psum")
        smax_ready = sem("smax_ready")
        maxT_psum = sem("maxT_psum")
        chi_ready = sem("chi_ready")
        clo_ready = sem("clo_ready")
        crow_in = sem("crow_in")
        st_psum = sem("st_psum")
        p_ready = sem("p_ready")
        pv_psum = sem("pv_psum")
        pv_ready = sem("pv_ready")
        rsum_ready = sem("rsum_ready")
        rsum16_ready = sem("rsum16_ready")
        rpair_ready = sem("rpair_ready")
        r_psum = sem("r_psum")
        oT_ready = sem("oT_ready")
        ohi_ready = sem("ohi_ready")
        olo_ready = sem("olo_ready")
        o_psum = sem("o_psum")
        o_ready = sem("o_ready")
        stats2 = sem("stats2")
        mv2_ready = sem("mv2_ready")
        norm2 = sem("norm2")
        y_init = sem("y_init")
        y_beta = sem("y_beta")
        y_o = sem("y_o")
        tg_ready = sem("tg_ready")
        y_ready = sem("y_ready")
        stored = sem("stored")
        pool_zero = sem("pool_zero")
        ms_rows = sem("ms_rows")

        xg = x.rearrange("(g b) n d -> g n b d", b=G)
        og = out.rearrange("(g b) n d -> g n b d", b=G)

        def wait(eng, s, value):
            if not isinstance(value, int) or value > 0:
                eng.wait_ge(s, value)

        def pipeline(eng, step):
            step(0, 0, True, False, False, True)
            step(1, 1, True, True, False, True)
            with eng.Fori(2, STEPS - 2, 2) as t:
                step(t, 0, True, True, True, True)
                step(t + 1, 1, True, True, True, True)
            step(STEPS - 2, 0, True, True, True, True)
            step(STEPS - 1, 1, True, True, True, False)
            step(STEPS, 0, False, True, True, False)
            step(STEPS + 1, 1, False, False, True, False)

        block = ctx.enter_context(nc.Block())

        @block.sync
        def _(sp):
            nc.sync.dma_start(x_sb[:, 0], xg[0]).then_inc(x_loaded, 16)
            nc.sync.dma_start(adj_sb[:], adj).then_inc(core_load, 16)
            nc.sync.dma_start(w_sb[:], w_qkv.rearrange("(c p) n -> p c n", p=P)).then_inc(core_load, 16)
            nc.sync.dma_start(wp_sb[:], w_proj.rearrange("(c p) n -> p c n", p=P)).then_inc(c_load, 16)
            nc.sync.dma_start(bias0_sb[:], bias0.rearrange("(p o) -> p o", o=1)).then_inc(c_load, 16)
            for vec, dst in ((gamma, gamma_sb), (beta, beta_sb), (b_proj, bproj_sb)):
                nc.sync.dma_start(dst[:], vec.rearrange("(o d) -> o d", o=1).to_broadcast([P, D])).then_inc(c_load, 16)

            def step(t, par, a, bc, d, prep):
                if bc:
                    for part, done in enumerate((chi_ready, clo_ready)):
                        sp.wait_ge(done, t)
                        row = stack[STACK + part:STACK + part + 1, 1 - par, 0].rearrange("p h b n -> p (h b) n")
                        nc.sync.dma_start(row, crow[:, part]).then_inc(crow_in, 16)
                if a:
                    for j in range(DC):
                        if j == 0:
                            wait(sp, st_psum, UNITS * (t - 1))
                        both = sp.snap(4 * t + 2 * j + 2) if not isinstance(t, int) else 4 * t + 2 * j + 2
                        wait(sp, qkhi_ready, both)
                        wait(sp, qklo_ready, both)
                        for i in range(HC):
                            head = slice(HD * i, HD * (i + 1))
                            high = bass.AP(pairs[:].tensor, HD * i * PAIRS + 2 * j * G * N,
                                           [[PAIRS, HD], [(2 * DC + 1) * G * N, 2], [1, G * N]])
                            for blk, src in enumerate((high, pairs[head, 0, j], pairs[head, 1, j])):
                                dst = stack[blk * HD:(blk + 1) * HD, par, :, HC * j + i]
                                nc.sync.dma_start(dst.rearrange("p s b n -> p s (b n)"), src).then_inc(stacked[j], 16)

            pipeline(sp, step)

        @block.tensor
        def _(pe):
            pe.wait_ge(core_load, 16 * 2)
            pe.wait_ge(pool_const, 1)
            nc.tensor.transpose(sc_ps[0][:, 0, :], adj_sb[:], identf[:]).then_inc(adjT_ps, 1)
            pe.wait_ge(pool_const, 3)
            pe.wait_ge(act_const, 2)
            pe.wait_ge(dve_const, 3)

            def transpose_h(t, b):
                pe.wait_ge(hhi_ready, 4 * t + b + 1)
                pe.wait_ge(hlo_ready, 4 * t + b + 1)
                if b < 2:
                    wait(pe, v_ready, 2 * t - 1 + b)
                else:
                    pe.wait_ge(hT_ready, 4 * t + b - 1)
                to = a_ps[b % 2][:].bitcast(F16)
                for i, (h, c) in enumerate(((h_hi, 0), (h_hi, 1), (h_lo, 0), (h_lo, 1))):
                    mm = nc.tensor.transpose(to[:, i * N:(i + 1) * N], h[:, b, c * P:(c + 1) * P], ident16[:])
                mm.then_inc(hT_psum, 1)

            def layer0(t, i):
                pe.wait_ge(qkhi_ready, 4 * t + i + 1)
                pe.wait_ge(qklo_ready, 4 * t + i + 1)
                for k, (w, h) in enumerate(((adjT_hi, h_hi), (adjT_hi, h_lo), (adjT_lo, h_hi))):
                    mm = nc.tensor.matmul(a_ps[i][:], w[:], h[:, 2 * i:2 * i + 2].rearrange("p b d -> p (b d)"),
                                          start=(k == 0), stop=(k == 2))
                mm.then_inc(a_psum, 1)

            def project_qk(t, c):
                if c == 0:
                    pe.wait_ge(hT_ready, 4 * t + 4)
                if c >= 2:
                    pe.wait_ge(amax_ready, 2 * t + c - 1)
                col = (c % 2) * D + (c // 2) * P
                k = 0
                for w, part in ((w_hi, 0), (w_hi, 1), (w_lo, 0)):
                    for dc in range(DC):
                        mm = nc.tensor.matmul(a_ps[c % 2][:], w[:, dc, col:col + P],
                                              hT[:, part, dc].rearrange("p b n -> p (b n)"),
                                              start=(k == 0), stop=(k == 5))
                        k += 1
                mm.then_inc(qk_psum, 1)

            def project_v(t, i):
                pe.wait_ge(qkhi_ready, 4 * t + 3 + i)
                pe.wait_ge(qklo_ready, 4 * t + 3 + i)
                for bb in range(2):
                    k = 0
                    for part, w in ((0, w_hi), (1, w_hi), (0, w_lo)):
                        for dc in range(DC):
                            mm = nc.tensor.matmul(a_ps[i][:, bb * D:(bb + 1) * D], hT[:, part, dc, 2 * i + bb],
                                                  w[:, dc, 2 * D:3 * D], start=(k == 0), stop=(k == 5))
                            k += 1
                mm.then_inc(v_psum, 1)

            def scores(g, par, u):
                j, b = u // G, u % G
                if b == 0:
                    pe.wait_ge(stacked[j], 16 * DMAS * (g + 1))
                if u < SC_SLOTS:
                    wait(pe, p_ready, UNITS * (g - 1) + (8, 6, 7)[u])
                else:
                    pe.wait_ge(smax_ready, UNITS * g + u - SC_SLOTS + 1)
                to = sc_ps[u % SC_SLOTS]
                nc.tensor.matmul(to[:].rearrange("p h n -> p (h n)"), identb[:],
                                 mask_q[:].rearrange("p h n -> p (h n)"), start=True, stop=False, skip_group_check=True)
                for i in range(HC):
                    h = HC * j + i
                    mm = nc.tensor.matmul(to[:, i], stack[0:STACK, par, 0, h, b], stack[0:STACK, par, 1, h, b],
                                          start=False, stop=True, skip_group_check=True)
                mm.then_inc(s_psum, 1)

            def transpose_max(g):
                pe.wait_ge(smax_ready, UNITS * (g + 1))
                wait(pe, rsum_ready, g)
                nc.tensor.transpose(sum_ps[0:H * G, 1, :], smax[:].rearrange("p h b -> p (h b)"),
                                    identf[:]).then_inc(maxT_psum, 1)

            def scores_T(g, par, u):
                b, j = u // DC, u % DC
                if u == 0:
                    pe.wait_ge(crow_in, 32 * (g + 1))
                if u < SC_SLOTS:
                    pe.wait_ge(smax_ready, UNITS * g + 6 + u)
                else:
                    pe.wait_ge(p_ready, UNITS * g + u - SC_SLOTS + 1)
                to = sc_ps[(UNITS + u) % SC_SLOTS]
                nc.tensor.matmul(to[:].rearrange("p h n -> p (h n)"), identb[:],
                                 mask_k[:].rearrange("p h n -> p (h n)"), start=True, stop=False, skip_group_check=True)
                for i in range(HC):
                    h = HC * j + i
                    mm = nc.tensor.matmul(to[:, i], stack[0:ROWS, par, 1, h, b], stack[0:ROWS, par, 0, h, b],
                                          start=False, stop=True, skip_group_check=True)
                mm.then_inc(st_psum, 1)

            def values(g, par, u):
                b, j = u // DC, u % DC
                pe.wait_ge(p_ready, UNITS * g + u + 1)
                if j == 0:
                    if b % 2 == 0:
                        pe.wait_ge(v_ready, 2 * g + b // 2 + 1)
                    wait(pe, pv_ready, G * g + b)
                if u == 0:
                    wait(pe, oT_ready, G * g)
                    wait(pe, rsum_ready, g)
                    pe.wait_ge(clo_ready, g + 1)
                for i in range(HC):
                    h = HC * j + i
                    nc.tensor.matmul(pv_ps[HD * i:HD * (i + 1), j], v_sb[:, par, b, HD * h:HD * (h + 1)],
                                     p_sb[:, u % P_SLOTS, i], start=True, stop=True)
                for i in range(HC):
                    mm = nc.tensor.matmul(sum_ps[HD * i:HD * (i + 1), 0], sel_sum[:, u], p_sb[:, u % P_SLOTS, i],
                                          start=(u == 0), stop=(u == UNITS - 1), skip_group_check=True)
                mm.then_inc(pv_psum, 1)

            def spread(g, b):
                if b == 0:
                    pe.wait_ge(rpair_ready, g + 1)
                    pe.wait_ge(pv_ready, G * (g + 1))
                else:
                    pe.wait_ge(oT_ready, G * g + b)
                for j in range(DC):
                    mm = nc.tensor.matmul(pv_ps[:, j], sel_row[:, b * DC + j].rearrange("p h d -> p (h d)"), rpair[:],
                                          start=True, stop=True)
                mm.then_inc(r_psum, 1)

            def project_o(g, b):
                pe.wait_ge(ohi_ready, G * g + b + 1)
                pe.wait_ge(olo_ready, G * g + b + 1)
                wait(pe, o_ready, G * g + b)
                nc.tensor.matmul(o_ps[:, 0], bias_ones[:], bp_rows[:], start=True, stop=False)
                for k, (o, w) in enumerate(((oT_hi, wp_hi), (oT_hi, wp_lo), (oT_lo, wp_hi))):
                    for j in range(DC):
                        mm = nc.tensor.matmul(o_ps[:, 0], o[:, b, j], w[:, j], start=False, stop=(k == 2 and j == DC - 1))
                mm.then_inc(o_psum, 1)

            ORDER = ("S0 T0 S1 T1 T2 T3 S2 R0 S3 R1 S4 S5 R2 O0 S6 O1 R3 S7 Q0 O2 M0 Q1 O3 "
                     "L0 L1 E0 E1 E2 Q2 P0 P1 Q3 E3 P2 E4 P3 E5 V0 E6 P4 V1 P5 E7 P6 P7").split()

            def step(t, par, a, bc, d, prep):
                if isinstance(t, int) and t == 1:
                    pe.wait_ge(pool_const, 7)
                    pe.wait_ge(act_const, ACT_CONST)
                    pe.wait_ge(dve_const, DVE_CONST)
                    pe.wait_ge(ms_rows, 2)
                for what in ORDER:
                    kind, i = what[0], int(what[1])
                    if kind == "T" and a:
                        transpose_h(t, i)
                    elif kind == "L" and a:
                        layer0(t, i)
                    elif kind == "Q" and a:
                        project_qk(t, i)
                    elif kind == "V" and a:
                        project_v(t, i)
                    elif kind == "S" and bc:
                        scores(t - 1, 1 - par, i)
                    elif kind == "M" and bc:
                        transpose_max(t - 1)
                    elif kind == "E" and bc:
                        scores_T(t - 1, 1 - par, i)
                    elif kind == "P" and bc:
                        values(t - 1, 1 - par, i)
                    elif kind == "R" and d:
                        spread(t - 2, i)
                    elif kind == "O" and d:
                        project_o(t - 2, i)

            pipeline(pe, step)

        @block.scalar
        def _(act):
            act.wait_ge(adjT_ps, 1)
            nc.scalar.activation(adjT_hi[:], sc_ps[0][:, 0, :], ACT.Copy, scale=WS).then_inc(act_const, 1)
            act.wait_ge(core_load, 16 * 2)
            nc.scalar.activation(w_hi[:], w_sb[:], ACT.Copy, scale=WS).then_inc(act_const, 1)

            def later_constants():
                act.wait_ge(c_load, 16 * 5)
                nc.scalar.activation(wp_hi[:], wp_sb[:], ACT.Copy, scale=WS).then_inc(act_const, 1)
                nc.scalar.activation(bp_parts[:, 0], bproj_sb[:], ACT.Copy).then_inc(act_const, 1)

            def h_high(t, b):
                act.wait_ge(z_ready, G * t + b + 1)
                if b == 0:
                    wait(act, a_psum, 2 * t)
                    wait(act, hT_psum, G * t)
                nc.scalar.activation(h_hi[:, b], z_sb[:, b], ACT.Relu).then_inc(hhi_ready, 1)

            def take_hT(t, b):
                act.wait_ge(hT_psum, G * t + b + 1)
                if b == 0:
                    wait(act, v_psum, 2 * t)
                nc.scalar.activation(hT[:, :, :, b, :],
                                     a_ps[b % 2][:].bitcast(F16)[:, 0:4 * N].rearrange("p (s c n) -> p s c n", s=2, c=DC),
                                     ACT.Copy).then_inc(hT_ready, 1)

            def layer0_numbers(t, par):
                act.wait_ge(amax_ready, 2 * (t + 1))
                nc.scalar.activation(l0[:, par], amax[:], ACT.Relu, bias=bias0_sb[:, 0:1],
                                     scale=1.0 / WS).then_inc(l0_ready, 1)

            def start_y(g, par, b):
                if b == 0:
                    act.wait_ge(l0_ready, g + 1)
                    wait(act, stored, 16 * (g - 1))
                nc.scalar.activation(y_sb[:, par, b], x_sb[:, par, b], ACT.Identity,
                                     bias=l0[:, par, b:b + 1]).then_inc(y_init, 1)

            def load_x(t, par):
                wait(act, y_init, G * (t - 1))
                nc.scalar.dma_start(x_sb[:, par], xg[t]).then_inc(x_loaded, 16)

            def take_v(t, par, i):
                act.wait_ge(v_psum, 2 * t + i + 1)
                nc.scalar.activation(v_sb[:, par, 2 * i:2 * i + 2].rearrange("p b d -> p (b d)"), a_ps[i][:],
                                     ACT.Copy).then_inc(v_ready, 1)

            def qk_high(t, c):
                act.wait_ge(qk_psum, 4 * t + c + 1)
                if c % 2 == 0:
                    wait(act, stacked[c // 2], 16 * DMAS * t)
                nc.scalar.activation(pairs[:, c % 2, c // 2, c % 2], a_ps[c % 2][:], ACT.Copy).then_inc(qkhi_ready, 1)

            def max_high(g):
                act.wait_ge(maxT_psum, g + 1)
                wait(act, crow_in, 32 * g)
                nc.scalar.activation(crow[:, 0], sum_ps[0:H * G, 1, :], ACT.Copy, scale=-1.0 / MS).then_inc(chi_ready, 1)

            def exps(g, u):
                act.wait_ge(st_psum, UNITS * g + u + 1)
                wait(act, pv_psum, UNITS * g + u - P_SLOTS + 1)
                nc.scalar.activation(p_sb[:, u % P_SLOTS], sc_ps[(UNITS + u) % SC_SLOTS][:], ACT.Exp,
                                     scale=SCALE).then_inc(p_ready, 1)

            def take_pv(g, b):
                act.wait_ge(pv_psum, UNITS * g + DC * (b + 1))
                if b == 0:
                    wait(act, oT_ready, G * g)
                nc.scalar.activation(pv_sb[:, b], pv_ps[:, 0:DC], ACT.Copy).then_inc(pv_ready, 1)

            def o_high(g, b):
                act.wait_ge(oT_ready, G * g + b + 1)
                if b == 0:
                    wait(act, o_psum, G * g)
                nc.scalar.activation(oT_hi[:, b], oT[:, b], ACT.Copy).then_inc(ohi_ready, 1)

            def take_o(g, b):
                act.wait_ge(o_psum, G * g + b + 1)
                if b == 0:
                    wait(act, y_o, G * g)
                    wait(act, tg_ready, G * g)
                nc.scalar.activation(o_sb[:, b], o_ps[:, 0], ACT.Copy, scale=1.0 / (OS * WS)).then_inc(o_ready, 1)

            ORDER = ("T0 T1 C0 C1 O0 C2 T2 T3 O1 Y0 C3 Q0 O2 M0 Y1 Q1 Y2 Y3 X0 E0 L0 "
                     "E1 E2 Q2 A0 O3 Q3 E3 H0 E4 A1 H1 H2 E5 E6 V0 A2 H3 E7 A3 V1").split()

            def step(t, par, a, bc, d, prep):
                for what in ORDER:
                    kind, i = what[0], int(what[1])
                    if kind == "Y" and bc:
                        start_y(t - 1, 1 - par, i)
                    elif kind == "T" and a:
                        take_hT(t, i)
                        if isinstance(t, int) and t == 0 and i == G - 1:
                            later_constants()
                            load_x(1, 1)
                    elif kind == "L" and a:
                        layer0_numbers(t, par)
                    elif kind == "Q" and a:
                        qk_high(t, i)
                    elif kind == "V" and a:
                        take_v(t, par, i)
                    elif kind == "M" and bc:
                        max_high(t - 1)
                    elif kind == "E" and bc:
                        exps(t - 1, i)
                    elif kind == "A" and bc:
                        take_pv(t - 1, i)
                    elif kind == "O" and d:
                        take_o(t - 2, i)
                    elif kind == "C" and d:
                        o_high(t - 2, i)
                    elif kind == "X" and prep and not (isinstance(t, int) and t == 0):
                        load_x(t + 1, 1 - par)
                    elif kind == "H" and prep:
                        h_high(t + 1, i)

            for b in range(G):
                h_high(0, b)
            pipeline(act, step)

        @block.vector
        def _(dve):
            nc.vector.memset(mhalf[:], -0.5).then_inc(dve_const, 1)

            def stats_x(t, par):
                dve.wait_ge(x_loaded, 16 * (t + 1))
                wait(dve, mv1_ready, G * t)
                for b in range(G):
                    nc.vector.bn_stats(st1[:, b], x_sb[:, par, b]).then_inc(stats1, 1)

            def aggregate_x(t):
                dve.wait_ge(stats1, G * (t + 1))
                wait(dve, norm1, 3 * t)
                nc.vector.memset(dve_cell[:, 0:1], 0.0)
                for b in range(G):
                    nc.vector.bn_aggr(mv1[:, b], st1[:, b]).then_inc(mv1_ready, 1)

            def h_low(t, b):
                dve.wait_ge(hhi_ready, G * t + b + 1)
                if b == 0:
                    wait(dve, a_psum, 2 * t)
                nc.vector.scalar_tensor_tensor(h_lo[:, b], z_sb[:, b], 0.0, h_hi[:, b], ALU.max,
                                               ALU.subtract).then_inc(hlo_ready, 1)

            def layer0_max(t, i):
                dve.wait_ge(a_psum, 2 * t + i + 1)
                if i == 0:
                    wait(dve, l0_ready, t)
                nc.vector.tensor_reduce(amax[:, 2 * i:2 * i + 2], a_ps[i][:].rearrange("p (b d) -> p b d", b=2), AX.X,
                                        ALU.max).then_inc(amax_ready, 1)

            def qk_low(t, c):
                dve.wait_ge(qkhi_ready, 4 * t + c + 1)
                if c % 2 == 0:
                    wait(dve, stacked[c // 2], 16 * DMAS * t)
                nc.vector.tensor_tensor(pairs[:, 1 - c % 2, c // 2, c % 2], a_ps[c % 2][:], pairs[:, c % 2, c // 2, c % 2],
                                        ALU.subtract).then_inc(qklo_ready, 1)

            def row_max(g, u):
                j, b = u // G, u % G
                dve.wait_ge(s_psum, UNITS * g + u + 1)
                if u == 0:
                    wait(dve, maxT_psum, g)
                nc.vector.tensor_reduce(smax[:, HC * j:HC * (j + 1), b], sc_ps[u % SC_SLOTS][:], AX.X,
                                        ALU.max).then_inc(smax_ready, 1)

            def max_low(g):
                dve.wait_ge(chi_ready, g + 1)
                wait(dve, crow_in, 32 * g)
                nc.vector.scalar_tensor_tensor(crow[:, 1], sum_ps[0:H * G, 1, :], -1.0 / MS, crow[:, 0], ALU.mult,
                                               ALU.subtract).then_inc(clo_ready, 1)

            def invert_sums(g, part):
                if part == 0:
                    dve.wait_ge(pv_psum, UNITS * (g + 1))
                    nc.vector.reciprocal(rsum[:], sum_ps[:, 0, :]).then_inc(rsum_ready, 1)
                elif part == 1:
                    dve.wait_ge(rsum_ready, g + 1)
                    nc.vector.tensor_copy(rsum16[:], rsum[:]).then_inc(rsum16_ready, 1)
                else:
                    dve.wait_ge(rsum16_ready, g + 1)
                    wait(dve, r_psum, G * g)
                    nc.vector.scalar_tensor_tensor(rpair[:], rsum16[:], lo_rows[:, 0:1], rsum[:], ALU.mult,
                                                   ALU.add).then_inc(rpair_ready, 1)

            def scale_o(g, b):
                dve.wait_ge(r_psum, G * g + b + 1)
                dve.wait_ge(pv_ready, G * g + b + 1)
                if b == 0:
                    wait(dve, ohi_ready, G * g)
                    wait(dve, olo_ready, G * g)
                nc.vector.tensor_tensor(oT[:, b], pv_ps[:, 0:DC], pv_sb[:, b], ALU.mult).then_inc(oT_ready, 1)

            def stats_o(g, b):
                dve.wait_ge(o_ready, G * g + b + 1)
                nc.vector.bn_stats(st2[:, b], o_sb[:, b]).then_inc(stats2, 1)

            def aggregate_o(g):
                dve.wait_ge(stats2, G * (g + 1))
                wait(dve, norm2, 2 * g)
                wait(dve, tg_ready, G * g)
                nc.vector.memset(dve_cell[:, 1:2], 0.0)
                for b in range(G):
                    nc.vector.bn_aggr(mv2[:, b], st2[:, b]).then_inc(mv2_ready, 1)

            def finish(g, par, i):
                if i == 0:
                    dve.wait_ge(mv2_ready, G * (g + 1))
                    wait(dve, y_ready, G * g)
                if i == 1:
                    dve.wait_ge(norm2, 2 * (g + 1))
                for b in (i // 2 * 2, i // 2 * 2 + 1):
                    if i % 2 == 0:
                        nc.vector.scalar_tensor_tensor(t_sb[:, b], o_sb[:, b], mv2[:, b, 0:1], gamma_sb[:],
                                                       ALU.subtract, ALU.mult).then_inc(tg_ready, 1)
                    else:
                        dve.wait_ge(tg_ready, G * g + b + 1)
                        dve.wait_ge(y_o, G * g + b + 1)
                        nc.vector.scalar_tensor_tensor(y_sb[:, par, b], t_sb[:, b], rstd2[:, b:b + 1],
                                                       y_sb[:, par, b], ALU.mult, ALU.add).then_inc(y_ready, 1)

            ORDER = ("I0 I1 S0 I2 S1 O0 S2 O1 S3 S4 O2 S5 S6 B0 O3 S7 M0 Q0 Q1 "
                     "L0 L1 X0 X1 Q2 Q3 B1 B2 B3 G0 H0 H1 H2 F0 F1 F2 H3 F3").split()

            def step(t, par, a, bc, d, prep):
                for what in ORDER:
                    kind, i = what[0], int(what[1])
                    if kind == "I" and d:
                        invert_sums(t - 2, i)
                    elif kind == "O" and d:
                        scale_o(t - 2, i)
                    elif kind == "B" and d:
                        stats_o(t - 2, i)
                    elif kind == "G" and d:
                        aggregate_o(t - 2)
                    elif kind == "F" and d:
                        finish(t - 2, par, i)
                    elif kind == "S" and bc:
                        row_max(t - 1, i)
                    elif kind == "M" and bc:
                        max_low(t - 1)
                    elif kind == "L" and a:
                        layer0_max(t, i)
                    elif kind == "Q" and a:
                        qk_low(t, i)
                    elif kind == "X" and prep:
                        if i == 0:
                            stats_x(t + 1, 1 - par)
                        else:
                            aggregate_x(t + 1)
                    elif kind == "H" and prep:
                        h_low(t + 1, i)

            def split_core():
                dve.wait_ge(adjT_ps, 1)
                dve.wait_ge(act_const, 1)
                nc.vector.scalar_tensor_tensor(adjT_lo[:], sc_ps[0][:, 0, :], WS, adjT_hi[:], ALU.mult,
                                               ALU.subtract).then_inc(dve_const, 1)
                dve.wait_ge(core_load, 16 * 2)
                dve.wait_ge(act_const, 2)
                nc.vector.scalar_tensor_tensor(w_lo[:], w_sb[:], WS, w_hi[:], ALU.mult,
                                               ALU.subtract).then_inc(dve_const, 1)

            def later_constants():
                nc.vector.memset(bias_ones[:], OS * WS).then_inc(dve_const, 1)
                nc.vector.memset(bp_rows[:], 0.0).then_inc(dve_const, 1)
                for i in range(HC):
                    nc.vector.tensor_scalar(mask_q[:, i], adj_sb[:], 0.0, MASKED, ALU.is_equal,
                                            ALU.mult).then_inc(dve_const, 1)
                for i in range(HC):
                    nc.vector.tensor_scalar(mask_k[:, i], sc_ps[0][:, 0, :], 0.0, MASKED, ALU.is_equal,
                                            ALU.mult).then_inc(dve_const, 1)
                dve.wait_ge(c_load, 16 * 5)
                dve.wait_ge(act_const, 3)
                nc.vector.scalar_tensor_tensor(wp_lo[:], wp_sb[:], WS, wp_hi[:], ALU.mult,
                                               ALU.subtract).then_inc(dve_const, 1)
                dve.wait_ge(pool_const, 7)
                nc.vector.tensor_reduce(lo_rows[:], lo_pick[:].rearrange("p h u -> p (h u)"), AX.X,
                                        ALU.add).then_inc(dve_const, 1)
                dve.wait_ge(act_const, 4)
                nc.vector.tensor_tensor(bproj_r1[:], bproj_sb[:], bp_parts[:, 0], ALU.subtract).then_inc(dve_const, 1)
                dve.wait_ge(dve_const, DVE_CONST - 6)
                nc.vector.tensor_copy(bp_parts[:, 1], bproj_r1[:]).then_inc(dve_const, 1)
                dve.wait_ge(dve_const, DVE_CONST - 5)
                nc.vector.tensor_tensor(bproj_r2[:], bproj_r1[:], bp_parts[:, 1], ALU.subtract).then_inc(dve_const, 1)
                dve.wait_ge(dve_const, DVE_CONST - 4)
                nc.vector.tensor_copy(bp_parts[:, 2], bproj_r2[:]).then_inc(dve_const, 1)
                dve.wait_ge(dve_const, DVE_CONST - 3)
                for i in range(3):
                    nc.vector.tensor_copy(bp_rows[HD * i:HD * i + 1], bp_parts[HD * i:HD * i + 1, i]).then_inc(dve_const, 1)

            stats_x(0, 0)
            aggregate_x(0)
            split_core()
            for b in range(G):
                h_low(0, b)
            later_constants()
            pipeline(dve, step)

        @block.gpsimd
        def _(pool):
            for i, m in enumerate((identf, ident16, identb)):
                nc.gpsimd.memset(m[:], 0.0).then_inc(pool_zero, 1)
                pool.wait_ge(pool_zero, i + 1)
                nc.gpsimd.affine_select(out=m[:], in_=m[:], compare_op=ALU.not_equal, fill=1.0, base=0,
                                        pattern=[[-1, P]], channel_multiplier=1).then_inc(pool_const, 1)

            def carry_waits(cell):
                nc.gpsimd.tensor_tensor(pool_cell[:, cell:cell + 1], pool_cell[:, 0:1], pool_cell[:, 0:1], ALU.add)

            def invert_std_x(t):
                pool.wait_ge(mv1_ready, G * (t + 1))
                wait(pool, z_ready, G * t)
                carry_waits(1)
                nc.gpsimd.tensor_scalar(negm1[:], mv1[:, :, 0], -1.0, 0.0, ALU.mult, ALU.add).then_inc(norm1, 1)
                nc.gpsimd.tensor_scalar(ve1[:], mv1[:, :, 1], 1.0, EPS, ALU.mult, ALU.add).then_inc(norm1, 1)
                pool.wait_ge(norm1, 3 * t + 2)
                nc.gpsimd.tensor_tensor(rstd1[:], ve1[:], mhalf[:], ALU.pow).then_inc(norm1, 1)

            def normalise_x(t, par, b):
                if b == 0:
                    pool.wait_ge(norm1, 3 * t + 3)
                    wait(pool, hhi_ready, G * t)
                    wait(pool, hlo_ready, G * t)
                    carry_waits(2)
                nc.gpsimd.tensor_scalar(z_sb[:, b], x_sb[:, par, b], negm1[:, b:b + 1], rstd1[:, b:b + 1],
                                        ALU.add, ALU.mult).then_inc(z_ready, 1)

            def o_low(g, b):
                pool.wait_ge(ohi_ready, G * g + b + 1)
                if b == 0:
                    wait(pool, o_psum, G * g)
                nc.gpsimd.tensor_tensor(oT_lo[:, b], oT[:, b], oT_hi[:, b], ALU.subtract).then_inc(olo_ready, 1)

            def add_beta(g, par, b):
                if b == 0:
                    pool.wait_ge(y_init, G * (g + 1))
                nc.gpsimd.tensor_tensor(y_sb[:, par, b], y_sb[:, par, b], beta_sb[:], ALU.add).then_inc(y_beta, 1)

            def add_o(g, par, b):
                pool.wait_ge(o_ready, G * g + b + 1)
                if b == 0:
                    pool.wait_ge(y_beta, G * (g + 1))
                nc.gpsimd.tensor_tensor(y_sb[:, par, b], y_sb[:, par, b], o_sb[:, b], ALU.add).then_inc(y_o, 1)

            def normalise_o(g):
                pool.wait_ge(mv2_ready, G * (g + 1))
                wait(pool, y_ready, G * g)
                carry_waits(3)
                nc.gpsimd.tensor_scalar(ve2[:], mv2[:, :, 1], 1.0, EPS, ALU.mult, ALU.add).then_inc(norm2, 1)
                pool.wait_ge(norm2, 2 * g + 1)
                nc.gpsimd.tensor_tensor(rstd2[:], ve2[:], mhalf[:], ALU.pow).then_inc(norm2, 1)

            def store(g, par):
                pool.wait_ge(y_ready, G * (g + 1))
                nc.gpsimd.dma_start(og[g], y_sb[:, par]).then_inc(stored, 16)

            ORDER = ("C0 C1 Y0 C2 C3 B0 Y1 B1 Y2 B2 "
                     "X0 Z0 B3 Z1 Z2 Y3 N0 Z3 D0").split()

            def step(t, par, a, bc, d, prep):
                for what in ORDER:
                    kind, i = what[0], int(what[1])
                    if kind == "C" and d:
                        o_low(t - 2, i)
                    elif kind == "Y" and d:
                        add_o(t - 2, par, i)
                    elif kind == "B" and bc:
                        add_beta(t - 1, 1 - par, i)
                    elif kind == "X" and prep:
                        invert_std_x(t + 1)
                    elif kind == "Z" and prep:
                        normalise_x(t + 1, 1 - par, i)
                    elif kind == "N" and d:
                        normalise_o(t - 2)
                    elif kind == "D" and d:
                        store(t - 2, par)

            def later_constants():
                nc.gpsimd.memset(sel_sum[:], 0.0).then_inc(pool_zero, 1)
                nc.gpsimd.memset(sel_row[:], 0.0).then_inc(pool_zero, 1)
                nc.gpsimd.memset(lo_pick[:], 0.0).then_inc(pool_zero, 1)
                pool.wait_ge(pool_zero, 7)
                v = sel_sum[:].rearrange("p u (r e) -> p u r e", e=UNITS)
                nc.gpsimd.affine_select(out=v, in_=v, compare_op=ALU.not_equal, fill=SUM_SEL, base=0,
                                        pattern=[[1, UNITS], [0, HD // UNITS], [-1, UNITS]],
                                        channel_multiplier=0).then_inc(pool_const, 1)
                for part in range(2):
                    nc.gpsimd.affine_select(out=sel_row[:], in_=sel_row[:], compare_op=ALU.not_equal, fill=ROW_SEL,
                                            base=-UNITS * part, pattern=[[-1, UNITS], [-HD, HC], [0, HD]],
                                            channel_multiplier=1).then_inc(pool_const, 1)
                    pool.wait_ge(pool_const, 5 + part)
                nc.gpsimd.affine_select(out=lo_pick[:], in_=lo_pick[:], compare_op=ALU.not_equal, fill=-1.0, base=-UNITS,
                                        pattern=[[-HD, HC], [-1, UNITS]], channel_multiplier=1).then_inc(pool_const, 1)
                pool.wait_ge(pool_const, 7)
                for par in range(2):
                    nc.gpsimd.memset(stack[STACK:ROWS, par, 1], MS).then_inc(ms_rows, 1)
                    pool.wait_ge(ms_rows, par + 1)

            nc.gpsimd.memset(pool_cell[:], 0.0).then_inc(pool_zero, 1)
            pool.wait_ge(pool_zero, 4)
            pool.wait_ge(dve_const, 1)
            invert_std_x(0)
            for b in range(G):
                normalise_x(0, 0, b)
            later_constants()
            pool.wait_ge(c_load, 16 * 5)
            pipeline(pool, step)
            pool.wait_ge(stored, 16 * STEPS)


_INS = ["x", "adj", "L0_gnn_b", "L1_gnn_w_qkv", "L1_gnn_w_proj", "L1_gnn_b_proj", "L1_gnn_ln_gamma", "L1_gnn_ln_beta"]


def kernel(**inputs):
    import concourse.bacc as bacc
    from concourse.bass_utils import run_bass_kernel_spmd

    nc = bacc.Bacc("TRN2", target_bir_lowering=False, num_devices=1)
    arrays, args = {}, []
    for name in _INS:
        a = np.ascontiguousarray(inputs[name])
        arrays[f"in_{name}"] = a
        args.append(nc.dram_tensor(f"in_{name}", a.shape, mybir.dt.from_np(a.dtype), kind="ExternalInput").ap())
    out = nc.dram_tensor("out", (B, N, D), mybir.dt.float32, kind="ExternalOutput").ap()
    build(nc, *args, out)
    r = run_bass_kernel_spmd(nc, [arrays], core_ids=[0])
    return r.results[0]["out"]
```
